# Optimizing a Trainium2 kernel written in Bass

```python
import numpy as np
import jax
import jax.numpy as jnp

def _softmax(x, axis=-1):
    return jax.nn.softmax(x, axis=axis)

def _gelu(x):
    return jax.nn.gelu(x, approximate=True)

def _silu(x):
    return jax.nn.silu(x)

def _sigmoid(x):
    return jax.nn.sigmoid(x)

def _layernorm(x, axis=-1, eps=1e-05):
    m = jnp.mean(x, axis=axis, keepdims=True)
    v = jnp.var(x, axis=axis, keepdims=True)
    return (x - m) / jnp.sqrt(v + eps)

def _scatter_add(tgt, idx, src, axis=0):
    return tgt.at[idx].add(src)

def _segment_sum(src, seg, n):
    return jax.ops.segment_sum(src, seg, n)
kernel_name = 'mk_decoder_preln_d4_seqx_r8_630389'

def setup_inputs(seed: int=0):
    np.random.seed(seed)
    _w = jnp.asarray

    def _rec_inputs():
        import jax
        import jax.numpy as jnp
        _rk = jax.random.key(seed)
        x = -0.0002928 + 1 * jax.random.normal(jax.random.fold_in(_rk, 1), (32, 64, 128), jnp.float32)
        _lenS = 64 - jax.random.randint(jax.random.fold_in(_rk, 7), (32,), 0, max(1, 64 // 4) + 1, jnp.int32)
        _lenS2 = 64 - jax.random.randint(jax.random.fold_in(_rk, 8), (32,), 0, max(1, 64 // 4) + 1, jnp.int32)
        _ctx_1024P = jax.random.normal(jax.random.fold_in(_rk, 11), (32, 16, 128), jnp.float32)
        _ctx_1024c = jax.random.dirichlet(jax.random.fold_in(_rk, 511), 0.3 * jnp.ones((16,), jnp.float32), (32, 64))
        _ctx_1024t = jnp.einsum('bsk,bkd->bsd', _ctx_1024c, _ctx_1024P)
        _ctx_1024t = _ctx_1024t * jax.lax.rsqrt(jnp.mean(jnp.square(_ctx_1024t)) + 1e-12) * 0.953939
        ctx_1024 = -1.39393e-06 + 0.999914 * (_ctx_1024t + 0.3 * jax.random.normal(jax.random.fold_in(_rk, 611), (32, 64, 128), jnp.float32))
        fside_BxSx3_0 = jax.random.uniform(jax.random.fold_in(_rk, 12), (32, 64, 3), jnp.float32, 0.0, 0.999943)
        return (x, ctx_1024, fside_BxSx3_0)
    x, ctx_1024, fside_BxSx3_0 = _rec_inputs()

    def _L0_attn_setup():
        import jax, jax.numpy as jnp
        import numpy as np
        EPS = 0.0001

        def mp_normalize(x, axis):
            red = int(np.prod([x.shape[a] for a in axis])) if isinstance(axis, (list, tuple)) else x.shape[axis]
            w = jnp.sqrt(jnp.sum(jnp.square(x.astype(jnp.float32)), axis=axis, keepdims=True))
            w = EPS + w / np.sqrt(red)
            return x / w.astype(x.dtype)

        def mp_linear(x, w, gain):
            fan_in = w.shape[1]
            wn = mp_normalize(w.astype(jnp.float32), axis=(1,)) * (gain / np.sqrt(fan_in))
            return jnp.einsum('bse,oe->bso', x, wn.astype(x.dtype))

        def attention(query, gain, w_q, w_k, w_v, w_o, num_heads=16, attn_balance=0.5):
            B, S, E = query.shape
            hd = E // num_heads
            res = query
            q = mp_linear(query, w_q, gain).reshape(B, S, num_heads, hd).transpose(0, 2, 1, 3)
            k = mp_linear(query, w_k, gain).reshape(B, S, num_heads, hd).transpose(0, 2, 1, 3)
            v = mp_linear(query, w_v, gain).reshape(B, S, num_heads, hd).transpose(0, 2, 1, 3)
            q = mp_normalize(q, axis=(3,))
            k = mp_normalize(k, axis=(3,))
            scores = jnp.einsum('bnsh,bnsk->bnhk', q, k / np.sqrt(S))
            attn = jax.nn.softmax(scores, axis=3)
            o = jnp.einsum('bnhk,bnsk->bnsh', attn, v)
            o = o.transpose(0, 2, 1, 3).reshape(B, S, E)
            out = mp_linear(o, w_o, gain)
            t = attn_balance
            return (res * (1.0 - t) + out * t) / np.sqrt((1 - t) ** 2 + t ** 2)
        key = jax.random.key(seed)
        ks = jax.random.split(key, 5)
        B, S, E = (4, 512, 128)
        return {'query': jax.random.normal(ks[0], (B, S, E), dtype=jnp.float32), 'gain': jnp.float32(1.0), 'w_q': jax.random.normal(ks[1], (E, E), dtype=jnp.float32), 'w_k': jax.random.normal(ks[2], (E, E), dtype=jnp.float32), 'w_v': jax.random.normal(ks[3], (E, E), dtype=jnp.float32), 'w_o': jax.random.normal(ks[4], (E, E), dtype=jnp.float32)}
    _L0_attn_all = _L0_attn_setup()
    _L0_attn_in = {k: v for k, v in _L0_attn_all.items() if k in ('gain', 'w_q', 'w_k', 'w_v', 'w_o')}
    del _L0_attn_all

    def _L0_xattn_setup():
        import jax, jax.numpy as jnp
        import numpy as np
        D_MODEL = 128
        N_HEADS = 16
        D_HEAD = D_MODEL // N_HEADS
        WINDOW = 128

        def _heads(x):
            B, S, _ = x.shape
            return x.reshape(B, S, N_HEADS, D_HEAD).transpose(0, 2, 1, 3)
        key = jax.random.key(seed)
        ks = jax.random.split(key, 11)
        B, S = (1, 512)
        s = 1.0 / np.sqrt(D_MODEL)
        return {'query': jax.random.normal(ks[0], (B, S, D_MODEL), jnp.float32), 'key': jax.random.normal(ks[1], (B, S, D_MODEL), jnp.float32), 'value': jax.random.normal(ks[2], (B, S, D_MODEL), jnp.float32), 'Wq': jax.random.normal(ks[3], (D_MODEL, D_MODEL), jnp.float32) * s, 'bq': jnp.zeros((D_MODEL,), jnp.float32), 'Wk': jax.random.normal(ks[4], (D_MODEL, D_MODEL), jnp.float32) * s, 'bk': jnp.zeros((D_MODEL,), jnp.float32), 'Wv': jax.random.normal(ks[5], (D_MODEL, D_MODEL), jnp.float32) * s, 'bv': jnp.zeros((D_MODEL,), jnp.float32), 'Wo': jax.random.normal(ks[6], (D_MODEL, D_MODEL), jnp.float32) * s, 'bo': jnp.zeros((D_MODEL,), jnp.float32)}
    _L0_xattn_all = _L0_xattn_setup()
    _L0_xattn_in = {k: v for k, v in _L0_xattn_all.items() if k in ('Wq', 'bq', 'Wk', 'bk', 'Wv', 'bv', 'Wo', 'bo')}
    del _L0_xattn_all

    def _L0_ffn_setup():
        import jax, jax.numpy as jnp
        import numpy as np
        DIM = 128
        HIDDEN = 384
        SCALE = 1.0 / 127.0

        def _dequant(w_int, dtype):
            return w_int.astype(dtype) * jnp.asarray(SCALE, dtype)
        key = jax.random.key(seed)
        k_x, k_g, k_u, k_d = jax.random.split(key, 4)
        x = jax.random.normal(k_x, (4, 256, DIM), dtype=jnp.float32)
        w_gate = jax.random.randint(k_g, (HIDDEN, DIM), -127, 128, dtype=jnp.int32)
        w_up = jax.random.randint(k_u, (HIDDEN, DIM), -127, 128, dtype=jnp.int32)
        w_down = jax.random.randint(k_d, (DIM, HIDDEN), -127, 128, dtype=jnp.int32)
        return {'x': x, 'w_gate': w_gate, 'w_up': w_up, 'w_down': w_down}
    _L0_ffn_all = _L0_ffn_setup()
    _L0_ffn_in = {k: v for k, v in _L0_ffn_all.items() if k in ('w_gate', 'w_up', 'w_down')}
    del _L0_ffn_all

    def _L1_attn_setup():
        import jax, jax.numpy as jnp
        import numpy as np
        HIDDEN = 128
        HEADS = 16
        HEAD = HIDDEN // HEADS

        def _ternary_weight(key, shape):
            g = jax.random.normal(key, shape, dtype=jnp.float32)
            return jnp.where(jnp.abs(g) < 0.6, 0.0, jnp.sign(g)).astype(jnp.float32)

        def _tlin(x, w, s, b):
            return jnp.einsum('bsh,oh->bso', x, w) * s + b
        key = jax.random.key(seed)
        ks = jax.random.split(key, 10)
        x = jax.random.normal(ks[0], (2, 256, HIDDEN), dtype=jnp.float32)
        d = {'x': x}
        names = ['q', 'k', 'v', 'o']
        for i, n in enumerate(names):
            d[f'w_{n}'] = _ternary_weight(ks[1 + i], (HIDDEN, HIDDEN))
            d[f's_{n}'] = jnp.float32(0.02)
            d[f'b_{n}'] = jax.random.normal(ks[5 + i], (HIDDEN,), dtype=jnp.float32) * 0.02
        return d
    _L1_attn_all = _L1_attn_setup()
    _L1_attn_in = {k: v for k, v in _L1_attn_all.items() if k in ('w_q', 's_q', 'b_q', 'w_k', 's_k', 'b_k', 'w_v', 's_v', 'b_v', 'w_o', 's_o', 'b_o')}
    del _L1_attn_all

    def _L1_xattn_setup():
        import jax, jax.numpy as jnp
        import numpy as np
        import math
        D = 128
        H = 16
        HD = D // H

        def _split_heads(x, B, L):
            return x.reshape(B, L, H, HD).transpose(0, 2, 1, 3)
        key = jax.random.key(seed)
        ks = jax.random.split(key, 12)
        B, L = (2, 256)
        s = 1.0 / math.sqrt(D)
        inp = {'q': jax.random.normal(ks[0], (B, L, D), jnp.float32), 'k': jax.random.normal(ks[1], (B, L, D), jnp.float32), 'v': jax.random.normal(ks[2], (B, L, D), jnp.float32), 'Wq': jax.random.normal(ks[3], (D, D), jnp.float32) * s, 'bq': jnp.zeros((D,), jnp.float32), 'Wk': jax.random.normal(ks[4], (D, D), jnp.float32) * s, 'bk': jnp.zeros((D,), jnp.float32), 'Wv': jax.random.normal(ks[5], (D, D), jnp.float32) * s, 'bv': jnp.zeros((D,), jnp.float32), 'Wo': jax.random.normal(ks[6], (D, D), jnp.float32) * s, 'bo': jnp.zeros((D,), jnp.float32), 'P': jax.random.normal(ks[7], (H, H), jnp.float32)}
        return inp
    _L1_xattn_all = _L1_xattn_setup()
    _L1_xattn_in = {k: v for k, v in _L1_xattn_all.items() if k in ('Wq', 'bq', 'Wk', 'bk', 'Wv', 'bv', 'Wo', 'bo', 'P')}
    del _L1_xattn_all

    def _L1_ffn_setup():
        import jax, jax.numpy as jnp
        import numpy as np
        BLOCK = 32
        W_BITS = 4
        ACT_BITS = 16

        def act_qdq(x):
            qmax = 2.0 ** (ACT_BITS - 1) - 1.0
            scale = jnp.maximum(jnp.max(jnp.abs(x)) / qmax, 1e-12)
            return jnp.clip(jnp.round(x / scale), -qmax - 1.0, qmax) * scale

        def fixed_qdq_u16(x):
            scale = 1.0 / 65536.0
            return jnp.clip(jnp.round(x / scale), 0.0, 65535.0) * scale

        def lpbq_dequant(w):
            O, I = w.shape
            qmax = 2.0 ** (W_BITS - 1) - 1.0
            wb = w.reshape(O, I // BLOCK, BLOCK)
            s = jnp.maximum(jnp.max(jnp.abs(wb), axis=-1, keepdims=True) / qmax, 1e-12)
            wq = jnp.clip(jnp.round(wb / s), -qmax - 1.0, qmax) * s
            return wq.reshape(O, I)
        key = jax.random.key(seed)
        k1, k2, k3, k4 = jax.random.split(key, 4)
        B, S, H, I = (2, 512, 128, 384)
        x = jax.random.normal(k1, (B, S, H), jnp.float32)
        w_gate = jax.random.normal(k2, (I, H), jnp.float32) * 0.02
        w_up = jax.random.normal(k3, (I, H), jnp.float32) * 0.02
        w_down = jax.random.normal(k4, (H, I), jnp.float32) * 0.02
        return {'x': x, 'w_gate': w_gate, 'w_up': w_up, 'w_down': w_down}
    _L1_ffn_all = _L1_ffn_setup()
    _L1_ffn_in = {k: v for k, v in _L1_ffn_all.items() if k in ('w_gate', 'w_up', 'w_down')}
    del _L1_ffn_all

    def _L2_attn_setup():
        import jax, jax.numpy as jnp
        import numpy as np
        N_HEAD = 16
        EPS = 1e-06

        def _linear_attention(q, k, v):
            B, H, D = (q.shape[1], q.shape[2], q.shape[3])

            def step(carry, qkv_t):
                S, z = carry
                qt, kt, vt = qkv_t
                S = S + kt[..., :, None] * vt[..., None, :]
                z = z + kt
                num = jnp.einsum('bhi,bhij->bhj', qt, S)
                den = jnp.sum(qt * z, axis=-1, keepdims=True)
                return ((S, z), num / (den + EPS))
            S0 = jnp.zeros((B, H, D, D), q.dtype)
            z0 = jnp.zeros((B, H, D), q.dtype)
            _, y = jax.lax.scan(step, (S0, z0), (q, k, v))
            return y
        key = jax.random.key(seed)
        k1, k2, k3 = jax.random.split(key, 3)
        B, T, C = (2, 256, 128)
        x = jax.random.normal(k1, (B, T, C), dtype=jnp.float32)
        w_attn = jax.random.normal(k2, (C, 3 * C), dtype=jnp.float32) * 0.02
        w_proj = jax.random.normal(k3, (C, C), dtype=jnp.float32) * 0.02
        return {'x': x, 'w_attn': w_attn, 'w_proj': w_proj}
    _L2_attn_all = _L2_attn_setup()
    _L2_attn_in = {k: v for k, v in _L2_attn_all.items() if k in ('w_attn', 'w_proj')}
    del _L2_attn_all

    def _L2_xattn_setup():
        import jax, jax.numpy as jnp
        import numpy as np
        EPS = 1e-05

        def layer_norm(x, g, b):
            mu = jnp.mean(x, axis=-1, keepdims=True)
            var = jnp.var(x, axis=-1, keepdims=True)
            return (x - mu) * jax.lax.rsqrt(var + EPS) * g + b
        key = jax.random.key(seed)
        ks = jax.random.split(key, 8)
        dim, heads, dim_head = (128, 16, 64)
        inner = heads * dim_head
        b, n, m = (8, 512, 64)
        s = dim ** (-0.5)
        return {'x': jax.random.normal(ks[0], (b, n, dim), jnp.float32), 'latents': jax.random.normal(ks[1], (b, m, dim), jnp.float32), 'ln_m_g': jnp.ones((dim,), jnp.float32), 'ln_m_b': jnp.zeros((dim,), jnp.float32), 'ln_l_g': jnp.ones((dim,), jnp.float32), 'ln_l_b': jnp.zeros((dim,), jnp.float32), 'Wq': jax.random.normal(ks[2], (dim, inner), jnp.float32) * s, 'Wkv': jax.random.normal(ks[3], (dim, 2 * inner), jnp.float32) * s, 'Wout': jax.random.normal(ks[4], (inner, dim), jnp.float32) * s}
    _L2_xattn_all = _L2_xattn_setup()
    _L2_xattn_in = {k: v for k, v in _L2_xattn_all.items() if k in ('ln_m_g', 'ln_m_b', 'ln_l_g', 'ln_l_b', 'Wq', 'Wkv', 'Wout')}
    del _L2_xattn_all

    def _L2_ffn_setup():
        import jax, jax.numpy as jnp
        import numpy as np
        B, S, D, O, E, R, TOP_K = (4, 128, 128, 128, 8, 16, 2)
        SCALING = 32.0 / 16.0
        NEG_INF = -1000000000.0
        key = jax.random.key(seed)
        ks = jax.random.split(key, 6)
        return {'x': jax.random.normal(ks[0], (B, S, D), jnp.float32), 'base_w': jax.random.normal(ks[1], (O, D), jnp.float32) * 0.02, 'base_b': jnp.zeros((O,), jnp.float32), 'lora_A': jax.random.normal(ks[2], (E, D, R), jnp.float32) * 0.02, 'lora_B': jax.random.normal(ks[3], (E, R, O), jnp.float32) * 0.02, 'router_w': jax.random.normal(ks[4], (E, D), jnp.float32) * 0.02, 'router_b': jnp.zeros((E,), jnp.float32)}
    _L2_ffn_all = _L2_ffn_setup()
    _L2_ffn_in = {k: v for k, v in _L2_ffn_all.items() if k in ('base_w', 'base_b', 'lora_A', 'lora_B', 'router_w', 'router_b')}
    del _L2_ffn_all

    def _L3_attn_setup():
        import jax, jax.numpy as jnp
        import numpy as np
        B, L, D, H = (2, 256, 128, 4)
        DV = D // H
        P = 5
        CHUNK = 32
        CONV_K = 4
        FIR_K = (3, 15, 64)

        def _dwconv(x, w):
            K = w.shape[1]
            xt = jnp.pad(jnp.transpose(x, (0, 2, 1)), ((0, 0), (0, 0), (K - 1, 0)))
            y = jax.lax.conv_general_dilated(xt, w[:, None, :], (1,), 'VALID', dimension_numbers=('NCH', 'OIH', 'NCH'), feature_group_count=w.shape[0])
            return jnp.transpose(y, (0, 2, 1))

        def _l2norm(x):
            return x * jax.lax.rsqrt(jnp.sum(x * x, -1, keepdims=True) + 1e-06)

        def _delta_rule_chunkwise(q, k, v, beta, chunk=CHUNK):
            b, h, Lp, dk = q.shape
            dv = v.shape[-1]
            n = Lp // chunk
            q = _l2norm(q)
            k = _l2norm(k)
            v = v * beta[..., None]
            kb = k * beta[..., None]
            r = lambda t: t.reshape(b, h, n, chunk, -1)
            q, k, v, kb = (r(q), r(k), r(v), r(kb))
            sw = lambda t: jnp.swapaxes(t, -1, -2)
            strict = jnp.tril(jnp.ones((chunk, chunk), bool), -1)
            attn = jnp.where(strict, -(kb @ sw(k)), 0.0)
            T = jnp.linalg.inv(jnp.eye(chunk, dtype=q.dtype) - attn)
            u = T @ v
            w = T @ kb
            incl = jnp.tril(jnp.ones((chunk, chunk), bool), 0)
            qs, ks, us, ws = (jnp.moveaxis(t, 2, 0) for t in (q, k, u, w))
            S0 = jnp.zeros((b, h, dk, dv), q.dtype)

            def step(S, inp):
                q_i, k_i, u0, w_i = inp
                local = jnp.where(incl, q_i @ sw(k_i), 0.0)
                u_i = u0 - w_i @ S
                o_i = q_i @ S + local @ u_i
                return (S + sw(k_i) @ u_i, o_i)
            S, o = jax.lax.scan(step, S0, (qs, ks, us, ws))
            return (jnp.moveaxis(o, 0, 2).reshape(b, h, Lp, dv), S)

        def _stats(t):
            m = jnp.mean(t, -1, keepdims=True)
            v = jnp.mean(t * t, -1, keepdims=True)
            a = jnp.mean(jnp.abs(t), -1, keepdims=True)
            nrm = jnp.sqrt(jnp.sum(t * t, -1, keepdims=True))
            s = jnp.concatenate([jnp.broadcast_to(x, t.shape) for x in (m, v, a, nrm)], -1)
            return s.reshape(t.shape[0], t.shape[1], -1)

        def _forward(hs, Wq, Wk, Wv, conv_q, conv_k, conv_v, Wb, fir_s, fir_m, fir_l, gW1, gb1, gW2, gb2, log_tau, eps_logit, norm_w, Wo):
            b, Ln, _ = hs.shape
            q = jax.nn.silu(_dwconv(hs @ Wq, conv_q))
            k = jax.nn.silu(_dwconv(hs @ Wk, conv_k))
            v = jax.nn.silu(_dwconv(hs @ Wv, conv_v))
            beta = jax.nn.sigmoid(hs @ Wb)
            bh = lambda t: jnp.transpose(t.reshape(b, Ln, H, -1), (0, 2, 1, 3))
            o_d, _ = _delta_rule_chunkwise(bh(q), bh(k), bh(v), jnp.transpose(beta, (0, 2, 1)))
            delta_path = jnp.transpose(o_d, (0, 2, 1, 3))
            paths = jnp.stack([_dwconv(v, fir_s).reshape(b, Ln, H, DV), _dwconv(v, fir_m).reshape(b, Ln, H, DV), _dwconv(v, fir_l).reshape(b, Ln, H, DV), delta_path, v.reshape(b, Ln, H, DV)], axis=3)
            stats_flat = jnp.concatenate([_stats(paths[..., p, :]) for p in range(P)], -1)
            gate_in = jnp.concatenate([hs, stats_flat], -1)
            logits = jax.nn.gelu(gate_in @ gW1 + gb1, approximate=False) @ gW2 + gb2
            logits = logits.reshape(b, Ln, H, P)
            tau = jax.nn.softplus(log_tau) + 0.5
            probs = jax.nn.softmax(logits / tau[:, None], -1)
            eps = jax.nn.sigmoid(eps_logit) * 0.2
            probs = probs * (1.0 - jnp.sum(eps, -1, keepdims=True)) + eps
            o = jnp.einsum('blhp,blhpd->blhd', probs, paths)
            o = o * jax.lax.rsqrt(jnp.mean(o * o, -1, keepdims=True) + 1e-05) * norm_w
            return o.reshape(b, Ln, D) @ Wo
        key = jax.random.key(seed)
        ks = jax.random.split(key, 14)
        lin = lambda kk, fan_in, shape: jax.random.normal(kk, shape, jnp.float32) / np.float32(np.sqrt(fan_in))

        def fir(kk, K):
            w = np.zeros((D, K), np.float32)
            w[:, -1] = 1.0
            return jnp.asarray(w) + 0.001 * jax.random.normal(kk, (D, K), jnp.float32)
        in_gate = D + 4 * DV * H * P
        HF = 2 * D
        gb2 = np.zeros((H * P,), np.float32)
        gb2[np.arange(H) * P + P - 1] = 1.0
        return {'hidden_states': jax.random.normal(ks[0], (B, L, D), jnp.float32), 'Wq': lin(ks[1], D, (D, D)), 'Wk': lin(ks[2], D, (D, D)), 'Wv': lin(ks[3], D, (D, D)), 'conv_q': lin(ks[4], CONV_K, (D, CONV_K)), 'conv_k': lin(ks[5], CONV_K, (D, CONV_K)), 'conv_v': lin(ks[6], CONV_K, (D, CONV_K)), 'Wb': lin(ks[7], D, (D, H)), 'fir_s': fir(ks[8], FIR_K[0]), 'fir_m': fir(ks[9], FIR_K[1]), 'fir_l': fir(ks[10], FIR_K[2]), 'gW1': lin(ks[11], in_gate, (in_gate, HF)), 'gb1': jnp.zeros((HF,), jnp.float32), 'gW2': lin(ks[12], HF, (HF, H * P)), 'gb2': jnp.asarray(gb2), 'log_tau': jnp.zeros((H,), jnp.float32), 'eps_logit': jnp.zeros((H, P), jnp.float32), 'norm_w': jnp.ones((DV,), jnp.float32), 'Wo': lin(ks[13], D, (D, D))}
    _L3_attn_all = _L3_attn_setup()
    _L3_attn_in = {k: v for k, v in _L3_attn_all.items() if k in ('Wq', 'Wk', 'Wv', 'conv_q', 'conv_k', 'conv_v', 'Wb', 'fir_s', 'fir_m', 'fir_l', 'gW1', 'gb1', 'gW2', 'gb2', 'log_tau', 'eps_logit', 'norm_w', 'Wo')}
    del _L3_attn_all

    def _L3_xattn_setup():
        import jax, jax.numpy as jnp
        import numpy as np
        DIM = 128
        NUM_HEADS = 16
        HEAD_DIM = DIM // NUM_HEADS
        N_PAIRS = HEAD_DIM // 2
        MIN_PERIOD = 0.01
        MAX_PERIOD = 1.0
        TWO_PI = 2.0 * np.pi
        _AXES = np.arange(N_PAIRS) % 3
        _PERIODS = np.geomspace(MIN_PERIOD, MAX_PERIOD, N_PAIRS).astype(np.float32)
        _INV_FREQ = (TWO_PI / _PERIODS).astype(np.float32)

        def rope_sincos(coords):
            ax = jnp.asarray(_AXES)
            inv_freq = jnp.asarray(_INV_FREQ)
            angles = coords[..., ax] * inv_freq
            return (jnp.sin(angles), jnp.cos(angles))

        def apply_rotary(t, sin, cos):
            sin = sin[:, None, :, :]
            cos = cos[:, None, :, :]
            t1, t2 = (t[..., :N_PAIRS], t[..., N_PAIRS:])
            return jnp.concatenate([t1 * cos - t2 * sin, t1 * sin + t2 * cos], axis=-1)
        key = jax.random.key(seed)
        ks = jax.random.split(key, 12)
        B, Tq, Tk = (4, 256, 256)
        s = 1.0 / np.sqrt(DIM)
        return {'x': jax.random.normal(ks[0], (B, Tq, DIM), jnp.float32), 'memory': jax.random.normal(ks[1], (B, Tk, DIM), jnp.float32), 'query_coords': jax.random.uniform(ks[2], (B, Tq, 3), jnp.float32), 'memory_coords': jax.random.uniform(ks[3], (B, Tk, 3), jnp.float32), 'Wq': jax.random.normal(ks[4], (DIM, DIM), jnp.float32) * s, 'bq': jnp.zeros((DIM,), jnp.float32), 'Wk': jax.random.normal(ks[5], (DIM, DIM), jnp.float32) * s, 'bk': jnp.zeros((DIM,), jnp.float32), 'Wv': jax.random.normal(ks[6], (DIM, DIM), jnp.float32) * s, 'bv': jnp.zeros((DIM,), jnp.float32), 'Wo': jax.random.normal(ks[7], (DIM, DIM), jnp.float32) * s, 'bo': jnp.zeros((DIM,), jnp.float32)}
    _L3_xattn_all = _L3_xattn_setup()
    _L3_xattn_in = {k: v for k, v in _L3_xattn_all.items() if k in ('Wq', 'bq', 'Wk', 'bk', 'Wv', 'bv', 'Wo', 'bo')}
    del _L3_xattn_all

    def _L3_ffn_setup():
        import jax, jax.numpy as jnp
        import numpy as np
        D = 128
        F = 128
        E = 8
        K = 2
        B, T = (2, 256)

        def _moe_forward(x, router_w, w1, w2, shared_gate_up, shared_down, shared_gate_w):
            b, t, d = x.shape
            xf = x.reshape(-1, d)
            n = xf.shape[0]
            logits = xf @ router_w
            probs = jax.nn.softmax(logits, axis=-1)
            topw, topi = jax.lax.top_k(probs, K)
            combine = jnp.zeros((n, E), dtype=probs.dtype).at[jnp.arange(n)[:, None], topi].add(topw)
            h = jax.nn.silu(jnp.einsum('nd,edf->nef', xf, w1))
            ye = jnp.einsum('nef,efd->ned', h, w2)
            routed = jnp.einsum('ne,ned->nd', combine, ye)
            gu = xf @ shared_gate_up
            gate, up = (gu[:, :F], gu[:, F:])
            shared = jax.nn.silu(gate) * up @ shared_down
            shared = jax.nn.sigmoid(xf @ shared_gate_w) * shared
            return (routed + shared).reshape(b, t, d)
        key = jax.random.key(seed)
        ks = jax.random.split(key, 7)
        std = 0.02
        x = jax.random.normal(ks[0], (B, T, D), dtype=jnp.float32)
        router_w = jax.random.normal(ks[1], (D, E), dtype=jnp.float32) * std
        w1 = jax.random.normal(ks[2], (E, D, F), dtype=jnp.float32) * std
        w2 = jax.random.normal(ks[3], (E, F, D), dtype=jnp.float32) * std
        shared_gate_up = jax.random.normal(ks[4], (D, 2 * F), dtype=jnp.float32) * std
        shared_down = jax.random.normal(ks[5], (F, D), dtype=jnp.float32) * std
        shared_gate_w = jax.random.normal(ks[6], (D, 1), dtype=jnp.float32) * std
        return {'x': x, 'router_w': router_w, 'w1': w1, 'w2': w2, 'shared_gate_up': shared_gate_up, 'shared_down': shared_down, 'shared_gate_w': shared_gate_w}
    _L3_ffn_all = _L3_ffn_setup()
    _L3_ffn_in = {k: v for k, v in _L3_ffn_all.items() if k in ('router_w', 'w1', 'w2', 'shared_gate_up', 'shared_down', 'shared_gate_w')}
    del _L3_ffn_all
    return {'x': x, 'ctx_1024': ctx_1024, 'fside_BxSx3_0': fside_BxSx3_0, 'L0_attn_gain': _L0_attn_in['gain'], 'L0_attn_w_q': _L0_attn_in['w_q'], 'L0_attn_w_k': _L0_attn_in['w_k'], 'L0_attn_w_v': _L0_attn_in['w_v'], 'L0_attn_w_o': _L0_attn_in['w_o'], 'L0_xattn_Wq': _L0_xattn_in['Wq'], 'L0_xattn_bq': _L0_xattn_in['bq'], 'L0_xattn_Wk': _L0_xattn_in['Wk'], 'L0_xattn_bk': _L0_xattn_in['bk'], 'L0_xattn_Wv': _L0_xattn_in['Wv'], 'L0_xattn_bv': _L0_xattn_in['bv'], 'L0_xattn_Wo': _L0_xattn_in['Wo'], 'L0_xattn_bo': _L0_xattn_in['bo'], 'L0_ffn_w_gate': _L0_ffn_in['w_gate'], 'L0_ffn_w_up': _L0_ffn_in['w_up'], 'L0_ffn_w_down': _L0_ffn_in['w_down'], 'L1_attn_w_q': _L1_attn_in['w_q'], 'L1_attn_s_q': _L1_attn_in['s_q'], 'L1_attn_b_q': _L1_attn_in['b_q'], 'L1_attn_w_k': _L1_attn_in['w_k'], 'L1_attn_s_k': _L1_attn_in['s_k'], 'L1_attn_b_k': _L1_attn_in['b_k'], 'L1_attn_w_v': _L1_attn_in['w_v'], 'L1_attn_s_v': _L1_attn_in['s_v'], 'L1_attn_b_v': _L1_attn_in['b_v'], 'L1_attn_w_o': _L1_attn_in['w_o'], 'L1_attn_s_o': _L1_attn_in['s_o'], 'L1_attn_b_o': _L1_attn_in['b_o'], 'L1_xattn_Wq': _L1_xattn_in['Wq'], 'L1_xattn_bq': _L1_xattn_in['bq'], 'L1_xattn_Wk': _L1_xattn_in['Wk'], 'L1_xattn_bk': _L1_xattn_in['bk'], 'L1_xattn_Wv': _L1_xattn_in['Wv'], 'L1_xattn_bv': _L1_xattn_in['bv'], 'L1_xattn_Wo': _L1_xattn_in['Wo'], 'L1_xattn_bo': _L1_xattn_in['bo'], 'L1_xattn_P': _L1_xattn_in['P'], 'L1_ffn_w_gate': _L1_ffn_in['w_gate'], 'L1_ffn_w_up': _L1_ffn_in['w_up'], 'L1_ffn_w_down': _L1_ffn_in['w_down'], 'L2_attn_w_attn': _L2_attn_in['w_attn'], 'L2_attn_w_proj': _L2_attn_in['w_proj'], 'L2_xattn_ln_m_g': _L2_xattn_in['ln_m_g'], 'L2_xattn_ln_m_b': _L2_xattn_in['ln_m_b'], 'L2_xattn_ln_l_g': _L2_xattn_in['ln_l_g'], 'L2_xattn_ln_l_b': _L2_xattn_in['ln_l_b'], 'L2_xattn_Wq': _L2_xattn_in['Wq'], 'L2_xattn_Wkv': _L2_xattn_in['Wkv'], 'L2_xattn_Wout': _L2_xattn_in['Wout'], 'L2_ffn_base_w': _L2_ffn_in['base_w'], 'L2_ffn_base_b': _L2_ffn_in['base_b'], 'L2_ffn_lora_A': _L2_ffn_in['lora_A'], 'L2_ffn_lora_B': _L2_ffn_in['lora_B'], 'L2_ffn_router_w': _L2_ffn_in['router_w'], 'L2_ffn_router_b': _L2_ffn_in['router_b'], 'L3_attn_Wq': _L3_attn_in['Wq'], 'L3_attn_Wk': _L3_attn_in['Wk'], 'L3_attn_Wv': _L3_attn_in['Wv'], 'L3_attn_conv_q': _L3_attn_in['conv_q'], 'L3_attn_conv_k': _L3_attn_in['conv_k'], 'L3_attn_conv_v': _L3_attn_in['conv_v'], 'L3_attn_Wb': _L3_attn_in['Wb'], 'L3_attn_fir_s': _L3_attn_in['fir_s'], 'L3_attn_fir_m': _L3_attn_in['fir_m'], 'L3_attn_fir_l': _L3_attn_in['fir_l'], 'L3_attn_gW1': _L3_attn_in['gW1'], 'L3_attn_gb1': _L3_attn_in['gb1'], 'L3_attn_gW2': _L3_attn_in['gW2'], 'L3_attn_gb2': _L3_attn_in['gb2'], 'L3_attn_log_tau': _L3_attn_in['log_tau'], 'L3_attn_eps_logit': _L3_attn_in['eps_logit'], 'L3_attn_norm_w': _L3_attn_in['norm_w'], 'L3_attn_Wo': _L3_attn_in['Wo'], 'L3_xattn_Wq': _L3_xattn_in['Wq'], 'L3_xattn_bq': _L3_xattn_in['bq'], 'L3_xattn_Wk': _L3_xattn_in['Wk'], 'L3_xattn_bk': _L3_xattn_in['bk'], 'L3_xattn_Wv': _L3_xattn_in['Wv'], 'L3_xattn_bv': _L3_xattn_in['bv'], 'L3_xattn_Wo': _L3_xattn_in['Wo'], 'L3_xattn_bo': _L3_xattn_in['bo'], 'L3_ffn_router_w': _L3_ffn_in['router_w'], 'L3_ffn_w1': _L3_ffn_in['w1'], 'L3_ffn_w2': _L3_ffn_in['w2'], 'L3_ffn_shared_gate_up': _L3_ffn_in['shared_gate_up'], 'L3_ffn_shared_down': _L3_ffn_in['shared_down'], 'L3_ffn_shared_gate_w': _L3_ffn_in['shared_gate_w']}

def reference(x, ctx_1024, fside_BxSx3_0, L0_attn_gain, L0_attn_w_q, L0_attn_w_k, L0_attn_w_v, L0_attn_w_o, L0_xattn_Wq, L0_xattn_bq, L0_xattn_Wk, L0_xattn_bk, L0_xattn_Wv, L0_xattn_bv, L0_xattn_Wo, L0_xattn_bo, L0_ffn_w_gate, L0_ffn_w_up, L0_ffn_w_down, L1_attn_w_q, L1_attn_s_q, L1_attn_b_q, L1_attn_w_k, L1_attn_s_k, L1_attn_b_k, L1_attn_w_v, L1_attn_s_v, L1_attn_b_v, L1_attn_w_o, L1_attn_s_o, L1_attn_b_o, L1_xattn_Wq, L1_xattn_bq, L1_xattn_Wk, L1_xattn_bk, L1_xattn_Wv, L1_xattn_bv, L1_xattn_Wo, L1_xattn_bo, L1_xattn_P, L1_ffn_w_gate, L1_ffn_w_up, L1_ffn_w_down, L2_attn_w_attn, L2_attn_w_proj, L2_xattn_ln_m_g, L2_xattn_ln_m_b, L2_xattn_ln_l_g, L2_xattn_ln_l_b, L2_xattn_Wq, L2_xattn_Wkv, L2_xattn_Wout, L2_ffn_base_w, L2_ffn_base_b, L2_ffn_lora_A, L2_ffn_lora_B, L2_ffn_router_w, L2_ffn_router_b, L3_attn_Wq, L3_attn_Wk, L3_attn_Wv, L3_attn_conv_q, L3_attn_conv_k, L3_attn_conv_v, L3_attn_Wb, L3_attn_fir_s, L3_attn_fir_m, L3_attn_fir_l, L3_attn_gW1, L3_attn_gb1, L3_attn_gW2, L3_attn_gb2, L3_attn_log_tau, L3_attn_eps_logit, L3_attn_norm_w, L3_attn_Wo, L3_xattn_Wq, L3_xattn_bq, L3_xattn_Wk, L3_xattn_bk, L3_xattn_Wv, L3_xattn_bv, L3_xattn_Wo, L3_xattn_bo, L3_ffn_router_w, L3_ffn_w1, L3_ffn_w2, L3_ffn_shared_gate_up, L3_ffn_shared_down, L3_ffn_shared_gate_w):
    import jax
    import jax.numpy as jnp

    def _L0_attn_ref(query, gain, w_q, w_k, w_v, w_o):
        import jax, jax.numpy as jnp
        import numpy as np
        EPS = 0.0001

        def mp_normalize(x, axis):
            red = int(np.prod([x.shape[a] for a in axis])) if isinstance(axis, (list, tuple)) else x.shape[axis]
            w = jnp.sqrt(jnp.sum(jnp.square(x.astype(jnp.float32)), axis=axis, keepdims=True))
            w = EPS + w / np.sqrt(red)
            return x / w.astype(x.dtype)

        def mp_linear(x, w, gain):
            fan_in = w.shape[1]
            wn = mp_normalize(w.astype(jnp.float32), axis=(1,)) * (gain / np.sqrt(fan_in))
            return jnp.einsum('bse,oe->bso', x, wn.astype(x.dtype))

        def attention(query, gain, w_q, w_k, w_v, w_o, num_heads=16, attn_balance=0.5):
            B, S, E = query.shape
            hd = E // num_heads
            res = query
            q = mp_linear(query, w_q, gain).reshape(B, S, num_heads, hd).transpose(0, 2, 1, 3)
            k = mp_linear(query, w_k, gain).reshape(B, S, num_heads, hd).transpose(0, 2, 1, 3)
            v = mp_linear(query, w_v, gain).reshape(B, S, num_heads, hd).transpose(0, 2, 1, 3)
            q = mp_normalize(q, axis=(3,))
            k = mp_normalize(k, axis=(3,))
            scores = jnp.einsum('bnsh,bnsk->bnhk', q, k / np.sqrt(S))
            attn = jax.nn.softmax(scores, axis=3)
            o = jnp.einsum('bnhk,bnsk->bnsh', attn, v)
            o = o.transpose(0, 2, 1, 3).reshape(B, S, E)
            out = mp_linear(o, w_o, gain)
            t = attn_balance
            return (res * (1.0 - t) + out * t) / np.sqrt((1 - t) ** 2 + t ** 2)
        return attention(query, gain, w_q, w_k, w_v, w_o)

    def _L0_xattn_ref(query, key, value, Wq, bq, Wk, bk, Wv, bv, Wo, bo):
        import jax, jax.numpy as jnp
        import numpy as np
        D_MODEL = 128
        N_HEADS = 16
        D_HEAD = D_MODEL // N_HEADS
        WINDOW = 128

        def _heads(x):
            B, S, _ = x.shape
            return x.reshape(B, S, N_HEADS, D_HEAD).transpose(0, 2, 1, 3)
        B, S, _ = query.shape
        q = _heads(query @ Wq.T + bq)
        k = _heads(key @ Wk.T + bk)
        v = _heads(value @ Wv.T + bv)
        scores = jnp.einsum('bhqd,bhkd->bhqk', q, k) / np.sqrt(D_HEAD).astype(np.float32)
        idx = jnp.arange(S)
        local = jnp.abs(idx[:, None] - idx[None, :]) <= WINDOW // 2
        scores = jnp.where(local[None, None, :, :], scores, -jnp.inf)
        attn = jax.nn.softmax(scores, axis=-1)
        ctx = jnp.einsum('bhqk,bhkd->bhqd', attn, v)
        ctx = ctx.transpose(0, 2, 1, 3).reshape(B, S, D_MODEL)
        return ctx @ Wo.T + bo

    def _L0_ffn_ref(x, w_gate, w_up, w_down):
        import jax, jax.numpy as jnp
        import numpy as np
        DIM = 128
        HIDDEN = 384
        SCALE = 1.0 / 127.0

        def _dequant(w_int, dtype):
            return w_int.astype(dtype) * jnp.asarray(SCALE, dtype)
        wg = _dequant(w_gate, x.dtype)
        wu = _dequant(w_up, x.dtype)
        wd = _dequant(w_down, x.dtype)
        gate = jnp.einsum('bsd,hd->bsh', x, wg)
        up = jnp.einsum('bsd,hd->bsh', x, wu)
        h = jax.nn.silu(gate) * up
        return jnp.einsum('bsh,dh->bsd', h, wd)

    def _L1_attn_ref(x, w_q, s_q, b_q, w_k, s_k, b_k, w_v, s_v, b_v, w_o, s_o, b_o):
        import jax, jax.numpy as jnp
        import numpy as np
        HIDDEN = 128
        HEADS = 16
        HEAD = HIDDEN // HEADS

        def _ternary_weight(key, shape):
            g = jax.random.normal(key, shape, dtype=jnp.float32)
            return jnp.where(jnp.abs(g) < 0.6, 0.0, jnp.sign(g)).astype(jnp.float32)

        def _tlin(x, w, s, b):
            return jnp.einsum('bsh,oh->bso', x, w) * s + b
        B, S, H = x.shape

        def split_heads(t):
            return t.reshape(B, S, HEADS, HEAD).transpose(0, 2, 1, 3)
        q = split_heads(_tlin(x, w_q, s_q, b_q))
        k = split_heads(_tlin(x, w_k, s_k, b_k))
        v = split_heads(_tlin(x, w_v, s_v, b_v))
        scores = jnp.einsum('bhqd,bhkd->bhqk', q, k) / jnp.sqrt(jnp.float32(HEAD))
        attn = jax.nn.softmax(scores, axis=-1)
        ctx = jnp.einsum('bhqk,bhkd->bhqd', attn, v)
        ctx = ctx.transpose(0, 2, 1, 3).reshape(B, S, H)
        return _tlin(ctx, w_o, s_o, b_o)

    def _L1_xattn_ref(q, k, v, Wq, bq, Wk, bk, Wv, bv, Wo, bo, P):
        import jax, jax.numpy as jnp
        import numpy as np
        import math
        D = 128
        H = 16
        HD = D // H

        def _split_heads(x, B, L):
            return x.reshape(B, L, H, HD).transpose(0, 2, 1, 3)
        B, L, _ = q.shape
        qh = _split_heads(q @ Wq.T + bq, B, L)
        kh = _split_heads(k @ Wk.T + bk, B, L)
        vh = _split_heads(v @ Wv.T + bv, B, L)
        logits = jnp.einsum('bhld,bhmd->bhlm', qh, kh) / math.sqrt(HD)
        logits = jnp.einsum('bhlm,hg->bglm', logits, P)
        attn = jax.nn.softmax(logits, axis=-1)
        out = jnp.einsum('bhlm,bhmd->bhld', attn, vh)
        out = out.transpose(0, 2, 1, 3).reshape(B, L, D)
        return out @ Wo.T + bo

    def _L1_ffn_ref(x, w_gate, w_up, w_down):
        import jax, jax.numpy as jnp
        import numpy as np
        BLOCK = 32
        W_BITS = 4
        ACT_BITS = 16

        def act_qdq(x):
            qmax = 2.0 ** (ACT_BITS - 1) - 1.0
            scale = jnp.maximum(jnp.max(jnp.abs(x)) / qmax, 1e-12)
            return jnp.clip(jnp.round(x / scale), -qmax - 1.0, qmax) * scale

        def fixed_qdq_u16(x):
            scale = 1.0 / 65536.0
            return jnp.clip(jnp.round(x / scale), 0.0, 65535.0) * scale

        def lpbq_dequant(w):
            O, I = w.shape
            qmax = 2.0 ** (W_BITS - 1) - 1.0
            wb = w.reshape(O, I // BLOCK, BLOCK)
            s = jnp.maximum(jnp.max(jnp.abs(wb), axis=-1, keepdims=True) / qmax, 1e-12)
            wq = jnp.clip(jnp.round(wb / s), -qmax - 1.0, qmax) * s
            return wq.reshape(O, I)
        x = act_qdq(x)
        up = act_qdq(x @ lpbq_dequant(w_up).T)
        gate = act_qdq(x @ lpbq_dequant(w_gate).T)
        sig = fixed_qdq_u16(jax.nn.sigmoid(gate))
        gate = act_qdq(gate * sig)
        o = act_qdq(gate * up)
        return o @ lpbq_dequant(w_down).T

    def _L2_attn_ref(x, w_attn, w_proj):
        import jax, jax.numpy as jnp
        import numpy as np
        N_HEAD = 16
        EPS = 1e-06

        def _linear_attention(q, k, v):
            B, H, D = (q.shape[1], q.shape[2], q.shape[3])

            def step(carry, qkv_t):
                S, z = carry
                qt, kt, vt = qkv_t
                S = S + kt[..., :, None] * vt[..., None, :]
                z = z + kt
                num = jnp.einsum('bhi,bhij->bhj', qt, S)
                den = jnp.sum(qt * z, axis=-1, keepdims=True)
                return ((S, z), num / (den + EPS))
            S0 = jnp.zeros((B, H, D, D), q.dtype)
            z0 = jnp.zeros((B, H, D), q.dtype)
            _, y = jax.lax.scan(step, (S0, z0), (q, k, v))
            return y
        B, T, C = x.shape
        H = N_HEAD
        D = C // H
        qkv = x @ w_attn
        q, k, v = jnp.split(qkv, 3, axis=-1)

        def to_tbhd(a):
            return a.reshape(B, T, H, D).transpose(1, 0, 2, 3)
        q = jax.nn.elu(to_tbhd(q)) + 1.0
        k = jax.nn.elu(to_tbhd(k)) + 1.0
        v = to_tbhd(v)
        y = _linear_attention(q, k, v)
        y = y.transpose(1, 0, 2, 3).reshape(B, T, C)
        return y @ w_proj

    def _L2_xattn_ref(x, latents, ln_m_g, ln_m_b, ln_l_g, ln_l_b, Wq, Wkv, Wout):
        import jax, jax.numpy as jnp
        import numpy as np
        EPS = 1e-05

        def layer_norm(x, g, b):
            mu = jnp.mean(x, axis=-1, keepdims=True)
            var = jnp.var(x, axis=-1, keepdims=True)
            return (x - mu) * jax.lax.rsqrt(var + EPS) * g + b
        heads, dim_head = (16, 64)
        scale = dim_head ** (-0.5)
        x = layer_norm(x, ln_m_g, ln_m_b)
        lat = layer_norm(latents, ln_l_g, ln_l_b)
        b, m, _ = lat.shape
        q = lat @ Wq
        kv_input = jnp.concatenate([x, lat], axis=1)
        kv = kv_input @ Wkv
        k, v = jnp.split(kv, 2, axis=-1)

        def split_heads(t):
            return t.reshape(t.shape[0], t.shape[1], heads, dim_head).transpose(0, 2, 1, 3)
        q, k, v = (split_heads(q), split_heads(k), split_heads(v))
        dots = jnp.einsum('bhid,bhjd->bhij', q, k) * scale
        attn = jax.nn.softmax(dots, axis=-1)
        out = jnp.einsum('bhij,bhjd->bhid', attn, v)
        out = out.transpose(0, 2, 1, 3).reshape(b, m, heads * dim_head)
        return out @ Wout

    def _L2_ffn_ref(x, base_w, base_b, lora_A, lora_B, router_w, router_b):
        import jax, jax.numpy as jnp
        import numpy as np
        B, S, D, O, E, R, TOP_K = (4, 128, 128, 128, 8, 16, 2)
        SCALING = 32.0 / 16.0
        NEG_INF = -1000000000.0
        result = jnp.einsum('bsd,od->bso', x, base_w) + base_b
        ax = jnp.einsum('bsd,edr->bser', x, lora_A)
        bax = jnp.einsum('bser,ero->bseo', ax, lora_B)
        logits = jnp.einsum('bsd,ed->bse', x, router_w) + router_b
        kth = jax.lax.top_k(logits, TOP_K)[0][..., -1:]
        masked = jnp.where(logits < kth, NEG_INF, logits)
        expert_weights = jax.nn.softmax(masked, axis=-1)
        return result + SCALING * jnp.einsum('bse,bseo->bso', expert_weights, bax)

    def _L3_attn_ref(hidden_states, Wq, Wk, Wv, conv_q, conv_k, conv_v, Wb, fir_s, fir_m, fir_l, gW1, gb1, gW2, gb2, log_tau, eps_logit, norm_w, Wo):
        import jax, jax.numpy as jnp
        import numpy as np
        B, L, D, H = (2, 256, 128, 4)
        DV = D // H
        P = 5
        CHUNK = 32
        CONV_K = 4
        FIR_K = (3, 15, 64)

        def _dwconv(x, w):
            K = w.shape[1]
            xt = jnp.pad(jnp.transpose(x, (0, 2, 1)), ((0, 0), (0, 0), (K - 1, 0)))
            y = jax.lax.conv_general_dilated(xt, w[:, None, :], (1,), 'VALID', dimension_numbers=('NCH', 'OIH', 'NCH'), feature_group_count=w.shape[0])
            return jnp.transpose(y, (0, 2, 1))

        def _l2norm(x):
            return x * jax.lax.rsqrt(jnp.sum(x * x, -1, keepdims=True) + 1e-06)

        def _delta_rule_chunkwise(q, k, v, beta, chunk=CHUNK):
            b, h, Lp, dk = q.shape
            dv = v.shape[-1]
            n = Lp // chunk
            q = _l2norm(q)
            k = _l2norm(k)
            v = v * beta[..., None]
            kb = k * beta[..., None]
            r = lambda t: t.reshape(b, h, n, chunk, -1)
            q, k, v, kb = (r(q), r(k), r(v), r(kb))
            sw = lambda t: jnp.swapaxes(t, -1, -2)
            strict = jnp.tril(jnp.ones((chunk, chunk), bool), -1)
            attn = jnp.where(strict, -(kb @ sw(k)), 0.0)
            T = jnp.linalg.inv(jnp.eye(chunk, dtype=q.dtype) - attn)
            u = T @ v
            w = T @ kb
            incl = jnp.tril(jnp.ones((chunk, chunk), bool), 0)
            qs, ks, us, ws = (jnp.moveaxis(t, 2, 0) for t in (q, k, u, w))
            S0 = jnp.zeros((b, h, dk, dv), q.dtype)

            def step(S, inp):
                q_i, k_i, u0, w_i = inp
                local = jnp.where(incl, q_i @ sw(k_i), 0.0)
                u_i = u0 - w_i @ S
                o_i = q_i @ S + local @ u_i
                return (S + sw(k_i) @ u_i, o_i)
            S, o = jax.lax.scan(step, S0, (qs, ks, us, ws))
            return (jnp.moveaxis(o, 0, 2).reshape(b, h, Lp, dv), S)

        def _stats(t):
            m = jnp.mean(t, -1, keepdims=True)
            v = jnp.mean(t * t, -1, keepdims=True)
            a = jnp.mean(jnp.abs(t), -1, keepdims=True)
            nrm = jnp.sqrt(jnp.sum(t * t, -1, keepdims=True))
            s = jnp.concatenate([jnp.broadcast_to(x, t.shape) for x in (m, v, a, nrm)], -1)
            return s.reshape(t.shape[0], t.shape[1], -1)

        def _forward(hs, Wq, Wk, Wv, conv_q, conv_k, conv_v, Wb, fir_s, fir_m, fir_l, gW1, gb1, gW2, gb2, log_tau, eps_logit, norm_w, Wo):
            b, Ln, _ = hs.shape
            q = jax.nn.silu(_dwconv(hs @ Wq, conv_q))
            k = jax.nn.silu(_dwconv(hs @ Wk, conv_k))
            v = jax.nn.silu(_dwconv(hs @ Wv, conv_v))
            beta = jax.nn.sigmoid(hs @ Wb)
            bh = lambda t: jnp.transpose(t.reshape(b, Ln, H, -1), (0, 2, 1, 3))
            o_d, _ = _delta_rule_chunkwise(bh(q), bh(k), bh(v), jnp.transpose(beta, (0, 2, 1)))
            delta_path = jnp.transpose(o_d, (0, 2, 1, 3))
            paths = jnp.stack([_dwconv(v, fir_s).reshape(b, Ln, H, DV), _dwconv(v, fir_m).reshape(b, Ln, H, DV), _dwconv(v, fir_l).reshape(b, Ln, H, DV), delta_path, v.reshape(b, Ln, H, DV)], axis=3)
            stats_flat = jnp.concatenate([_stats(paths[..., p, :]) for p in range(P)], -1)
            gate_in = jnp.concatenate([hs, stats_flat], -1)
            logits = jax.nn.gelu(gate_in @ gW1 + gb1, approximate=False) @ gW2 + gb2
            logits = logits.reshape(b, Ln, H, P)
            tau = jax.nn.softplus(log_tau) + 0.5
            probs = jax.nn.softmax(logits / tau[:, None], -1)
            eps = jax.nn.sigmoid(eps_logit) * 0.2
            probs = probs * (1.0 - jnp.sum(eps, -1, keepdims=True)) + eps
            o = jnp.einsum('blhp,blhpd->blhd', probs, paths)
            o = o * jax.lax.rsqrt(jnp.mean(o * o, -1, keepdims=True) + 1e-05) * norm_w
            return o.reshape(b, Ln, D) @ Wo
        return _forward(hidden_states, Wq, Wk, Wv, conv_q, conv_k, conv_v, Wb, fir_s, fir_m, fir_l, gW1, gb1, gW2, gb2, log_tau, eps_logit, norm_w, Wo)

    def _L3_xattn_ref(x, memory, query_coords, memory_coords, Wq, bq, Wk, bk, Wv, bv, Wo, bo):
        import jax, jax.numpy as jnp
        import numpy as np
        DIM = 128
        NUM_HEADS = 16
        HEAD_DIM = DIM // NUM_HEADS
        N_PAIRS = HEAD_DIM // 2
        MIN_PERIOD = 0.01
        MAX_PERIOD = 1.0
        TWO_PI = 2.0 * np.pi
        _AXES = np.arange(N_PAIRS) % 3
        _PERIODS = np.geomspace(MIN_PERIOD, MAX_PERIOD, N_PAIRS).astype(np.float32)
        _INV_FREQ = (TWO_PI / _PERIODS).astype(np.float32)

        def rope_sincos(coords):
            ax = jnp.asarray(_AXES)
            inv_freq = jnp.asarray(_INV_FREQ)
            angles = coords[..., ax] * inv_freq
            return (jnp.sin(angles), jnp.cos(angles))

        def apply_rotary(t, sin, cos):
            sin = sin[:, None, :, :]
            cos = cos[:, None, :, :]
            t1, t2 = (t[..., :N_PAIRS], t[..., N_PAIRS:])
            return jnp.concatenate([t1 * cos - t2 * sin, t1 * sin + t2 * cos], axis=-1)
        B, Tq, _ = x.shape
        Tk = memory.shape[1]
        H, D = (NUM_HEADS, HEAD_DIM)

        def split_heads(t, T):
            return t.reshape(B, T, H, D).transpose(0, 2, 1, 3)
        q = split_heads(x @ Wq.T + bq, Tq)
        k = split_heads(memory @ Wk.T + bk, Tk)
        v = split_heads(memory @ Wv.T + bv, Tk)
        q_sin, q_cos = rope_sincos(query_coords)
        k_sin, k_cos = rope_sincos(memory_coords)
        q = apply_rotary(q, q_sin, q_cos)
        k = apply_rotary(k, k_sin, k_cos)
        scale = 1.0 / np.sqrt(D).astype(np.float32)
        scores = jnp.einsum('bhqd,bhkd->bhqk', q, k) * scale
        attn = jax.nn.softmax(scores, axis=-1)
        out = jnp.einsum('bhqk,bhkd->bhqd', attn, v)
        out = out.transpose(0, 2, 1, 3).reshape(B, Tq, H * D)
        return out @ Wo.T + bo

    def _L3_ffn_ref(x, router_w, w1, w2, shared_gate_up, shared_down, shared_gate_w):
        import jax, jax.numpy as jnp
        import numpy as np
        D = 128
        F = 128
        E = 8
        K = 2
        B, T = (2, 256)

        def _moe_forward(x, router_w, w1, w2, shared_gate_up, shared_down, shared_gate_w):
            b, t, d = x.shape
            xf = x.reshape(-1, d)
            n = xf.shape[0]
            logits = xf @ router_w
            probs = jax.nn.softmax(logits, axis=-1)
            topw, topi = jax.lax.top_k(probs, K)
            combine = jnp.zeros((n, E), dtype=probs.dtype).at[jnp.arange(n)[:, None], topi].add(topw)
            h = jax.nn.silu(jnp.einsum('nd,edf->nef', xf, w1))
            ye = jnp.einsum('nef,efd->ned', h, w2)
            routed = jnp.einsum('ne,ned->nd', combine, ye)
            gu = xf @ shared_gate_up
            gate, up = (gu[:, :F], gu[:, F:])
            shared = jax.nn.silu(gate) * up @ shared_down
            shared = jax.nn.sigmoid(xf @ shared_gate_w) * shared
            return (routed + shared).reshape(b, t, d)
        return _moe_forward(x, router_w, w1, w2, shared_gate_up, shared_down, shared_gate_w)
    x = x + _L0_attn_ref(_layernorm(x, axis=-1), L0_attn_gain, L0_attn_w_q, L0_attn_w_k, L0_attn_w_v, L0_attn_w_o)
    x = x + _L0_xattn_ref(_layernorm(x, axis=-1), ctx_1024, ctx_1024, L0_xattn_Wq, L0_xattn_bq, L0_xattn_Wk, L0_xattn_bk, L0_xattn_Wv, L0_xattn_bv, L0_xattn_Wo, L0_xattn_bo)
    x = x + _L0_ffn_ref(_layernorm(x, axis=-1), L0_ffn_w_gate, L0_ffn_w_up, L0_ffn_w_down)
    x = x + _L1_attn_ref(_layernorm(x, axis=-1), L1_attn_w_q, L1_attn_s_q, L1_attn_b_q, L1_attn_w_k, L1_attn_s_k, L1_attn_b_k, L1_attn_w_v, L1_attn_s_v, L1_attn_b_v, L1_attn_w_o, L1_attn_s_o, L1_attn_b_o)
    x = x + _L1_xattn_ref(_layernorm(x, axis=-1), ctx_1024, ctx_1024, L1_xattn_Wq, L1_xattn_bq, L1_xattn_Wk, L1_xattn_bk, L1_xattn_Wv, L1_xattn_bv, L1_xattn_Wo, L1_xattn_bo, L1_xattn_P)
    x = x + _L1_ffn_ref(_layernorm(x, axis=-1), L1_ffn_w_gate, L1_ffn_w_up, L1_ffn_w_down)
    x = x + _L2_attn_ref(_layernorm(x, axis=-1), L2_attn_w_attn, L2_attn_w_proj)
    x = x + _L2_xattn_ref(ctx_1024, _layernorm(x, axis=-1), L2_xattn_ln_m_g, L2_xattn_ln_m_b, L2_xattn_ln_l_g, L2_xattn_ln_l_b, L2_xattn_Wq, L2_xattn_Wkv, L2_xattn_Wout)
    x = x + _L2_ffn_ref(_layernorm(x, axis=-1), L2_ffn_base_w, L2_ffn_base_b, L2_ffn_lora_A, L2_ffn_lora_B, L2_ffn_router_w, L2_ffn_router_b)
    x = x + _L3_attn_ref(_layernorm(x, axis=-1), L3_attn_Wq, L3_attn_Wk, L3_attn_Wv, L3_attn_conv_q, L3_attn_conv_k, L3_attn_conv_v, L3_attn_Wb, L3_attn_fir_s, L3_attn_fir_m, L3_attn_fir_l, L3_attn_gW1, L3_attn_gb1, L3_attn_gW2, L3_attn_gb2, L3_attn_log_tau, L3_attn_eps_logit, L3_attn_norm_w, L3_attn_Wo)
    x = x + _L3_xattn_ref(_layernorm(x, axis=-1), ctx_1024, fside_BxSx3_0, fside_BxSx3_0, L3_xattn_Wq, L3_xattn_bq, L3_xattn_Wk, L3_xattn_bk, L3_xattn_Wv, L3_xattn_bv, L3_xattn_Wo, L3_xattn_bo)
    x = x + _L3_ffn_ref(_layernorm(x, axis=-1), L3_ffn_router_w, L3_ffn_w1, L3_ffn_w2, L3_ffn_shared_gate_up, L3_ffn_shared_down, L3_ffn_shared_gate_w)
    return x

_drawn_inputs = setup_inputs


def setup_inputs(seed=0):
    import zlib

    import numpy as np

    out = dict(_drawn_inputs(seed))
    spreads = {'L0_xattn_bq': (0.0, 0.397),
     'L0_xattn_bk': (0.0, 2.0),
     'L0_xattn_bv': (0.0, 0.1),
     'L0_xattn_bo': (0.0, 0.1),
     'L1_xattn_bq': (0.0, 0.8),
     'L1_xattn_bk': (0.0, 2.0),
     'L1_xattn_bv': (0.0, 0.8),
     'L1_xattn_bo': (0.0, 2.0),
     'L2_xattn_ln_m_g': (1.0, 0.6),
     'L2_xattn_ln_m_b': (0.0, 0.8),
     'L2_xattn_ln_l_g': (1.0, 0.6),
     'L2_xattn_ln_l_b': (0.0, 0.8),
     'L2_ffn_base_b': (0.0, 2.0),
     'L2_ffn_router_b': (0.0, 2.0),
     'L3_attn_gb1': (0.0, 0.8),
     'L3_attn_log_tau': (0.0, 0.8),
     'L3_attn_eps_logit': (0.0, 2.0),
     'L3_attn_norm_w': (1.0, 0.6),
     'L3_xattn_bq': (0.0, 0.8),
     'L3_xattn_bk': (0.0, 0.8),
     'L3_xattn_bv': (0.0, 2.0),
     'L3_xattn_bo': (0.0, 2.0)}
    factors = {'fside_BxSx3_0': 8.0,
     'L1_attn_w_q': 8.0,
     'L1_attn_b_q': 29.793,
     'L1_attn_w_k': 8.0,
     'L1_attn_b_k': 64.0,
     'L1_attn_w_v': 8.0,
     'L1_attn_b_v': 8.0,
     'L1_attn_w_o': 8.0,
     'L1_attn_b_o': 23.646,
     'L1_xattn_Wq': 8.0,
     'L1_xattn_Wk': 8.0,
     'L1_xattn_Wv': 8.0,
     'L1_xattn_Wo': 8.0,
     'L1_xattn_P': 8.0,
     'L1_ffn_w_gate': 8.0,
     'L1_ffn_w_up': 8.0,
     'L1_ffn_w_down': 8.0,
     'L2_attn_w_attn': 8.0,
     'L2_attn_w_proj': 8.0,
     'L2_xattn_Wq': 8.0,
     'L2_xattn_Wkv': 8.0,
     'L2_xattn_Wout': 8.0,
     'L2_ffn_base_w': 64.0,
     'L2_ffn_lora_A': 64.0,
     'L2_ffn_lora_B': 64.0,
     'L2_ffn_router_w': 64.0,
     'L3_attn_Wq': 64.0,
     'L3_attn_Wk': 64.0,
     'L3_attn_Wv': 8.0,
     'L3_attn_conv_q': 64.0,
     'L3_attn_conv_k': 64.0,
     'L3_attn_conv_v': 8.0,
     'L3_attn_Wb': 64.0,
     'L3_attn_fir_s': 64.0,
     'L3_attn_fir_m': 35.2,
     'L3_attn_fir_l': 45.251,
     'L3_attn_gW1': 64.0,
     'L3_attn_gW2': 64.0,
     'L3_attn_gb2': 8.0,
     'L3_attn_Wo': 8.0,
     'L3_xattn_Wq': 8.0,
     'L3_xattn_Wk': 8.0,
     'L3_xattn_Wv': 8.0,
     'L3_xattn_Wo': 8.0,
     'L3_ffn_router_w': 64.0,
     'L3_ffn_w1': 64.0,
     'L3_ffn_w2': 64.0,
     'L3_ffn_shared_gate_up': 64.0,
     'L3_ffn_shared_down': 64.0,
     'L3_ffn_shared_gate_w': 64.0}
    for name, (base, spread) in spreads.items():
        noise = np.random.default_rng([zlib.crc32(name.encode()), seed]).standard_normal(out[name].shape)
        drawn = base * np.exp(spread * noise) if base else spread * noise
        out[name] = jnp.asarray(drawn.astype(out[name].dtype))
    for name, factor in factors.items():
        out[name] = (out[name] * factor).astype(out[name].dtype)
    return out
```

```python
from contextlib import ExitStack

import numpy as np
import concourse.bass as bass
from concourse import mybir

ALU = mybir.AluOpType
ACT = mybir.ActivationFunctionType
AX = mybir.AxisListType.X
F32 = mybir.dt.float32
I32 = mybir.dt.int32

P = 128
SEQ = 64
B = 32
NTOK = B * SEQ
NT = NTOK // P
NS = 2
TS = 2
ST = TS * P
SQ = ST // SEQ
NITER = NT // (NS * TS)
H, HD = 16, 8
GR = 4
V9 = HD + 1
H2, D2 = 16, 64
KV2 = 2 * SEQ
HID = 384
NE = 8
RND = 1.5 * 2.0 ** 23
ARENA = 8704
PERIODS = np.geomspace(0.01, 1.0, 4).astype(np.float32)
INV_FREQ = (2.0 * np.pi / PERIODS).astype(np.float32)
PI_A, PI_B = 6.28125, 0.0019340515136718750
PI_C = float(2 * np.pi - PI_A - PI_B)


def constants():
    i = np.arange(P)[:, None]
    j = np.arange(P)[None, :]
    c = {}
    c["ident"] = (i == j)
    c["fold"] = (i % SEQ == np.arange(SEQ)[None, :])
    c["causal"] = (i % SEQ <= j % SEQ)
    c["within"] = (i // SEQ == j // SEQ) & (i <= j)
    for m in (1, 2, 4, 8, 16, 32):
        c[f"up{m}"] = (i // (2 * m) == j // (2 * m)) & ((j // m) % 2 == 1) & ((i // m) % 2 == 0)
    c["blocks"] = (i // 32 == j // 32)
    c["ident32"] = (i % 32 == np.arange(32)[None, :])
    c["head_bias"] = np.where(i // HD == j // HD, 0.0, -1e30)
    c["parity"] = ((i // HD) % 2 == np.arange(2)[None, :])
    c["pair"] = ((i // (2 * HD)) % 2 == np.arange(2)[None, :])
    c["headsel"] = (i // 32 == np.arange(4)[None, :])
    d = np.arange(P) % HD
    rows = np.arange(8)[:, None]
    c["sin_sel"] = np.pad(np.where(rows == d % 4, np.where(d < 4, -1.0, 1.0), 0.0), ((0, P - 8), (0, 0)))
    c["cos_sel"] = np.pad((rows - 4 == d % 4) * 1.0, ((0, P - 8), (0, 0)))
    k = np.arange(156)[None, :]
    c["statsel"] = (k - 76 == i // 32)
    e = np.arange(NE)
    c["before"] = np.broadcast_to((e[None, :] < e[:, None]).reshape(1, NE * NE), (P, NE * NE))
    c["half_neg"] = np.full((P, 8), -0.5)
    c["half_pos"] = np.full((P, 1), 0.5)
    c["round"] = np.full((P, 1), RND)
    c["half_pi"] = np.full((P, 1), np.pi / 2)
    c["one_row"] = np.ones((P, P))
    return {n: np.ascontiguousarray(a, dtype=np.float32) for n, a in c.items()}


def offsets(widths):
    at, n = {}, 0
    for name, w in widths:
        at[name] = (n, w)
        n += w
    return at, n


CONST_W = [(n, a.shape[1]) for n, a in constants().items()]
A_W = [("L0a_gain", 1)] + [(f"L0x_{n}", w) for n, w in (("Wq", P), ("Wk", P), ("Wv", P), ("Wo", P), ("bq", 1),
       ("bk", 1), ("bv", 1), ("bo", P))] + \
      [(f"L1a_{n}", w) for n, w in (("Wq", P), ("Wk", P), ("Wv", P), ("Wo", P), ("bq", 1), ("bk", 1), ("bv", 1),
       ("bo", P), ("sq", 1), ("sk", 1), ("sv", 1), ("so", 1))] + \
      [(f"L1x_{n}", w) for n, w in (("Wq", P), ("Wk", P), ("Wv", P), ("Wo", P), ("bq", 1), ("bk", 1), ("bv", 1),
       ("bo", P), ("P", H))]
RAW_W = [("L0a_w", 4 * P), ("L1f_w", 9 * P)]
C_W = [("L2a_w", 3 * P), ("L2a_Wo", P), ("L2x_mg", 1), ("L2x_mb", 1), ("L2x_lg", 1), ("L2x_lb", 1),
       ("L2x_Wq", 1024), ("L2x_Wkv", 2048), ("L2x_Wo", 1024),
       ("L2f_in", P + NE), ("L2f_base", P), ("L2f_B", P), ("L2f_bb", P), ("L2f_rb", NE),
       ("L3a_w", 3 * P), ("L3a_Wb", 4), ("L3a_conv", 12), ("L3a_fir", 82), ("L3a_gW1", 256), ("L3a_gb1", 2),
       ("L3a_gW2", 40), ("L3a_gb2", 20), ("L3a_tau", 4), ("L3a_eps", 20), ("L3a_nw", 32), ("L3a_Wo", P),
       ("L3x_Wq", P), ("L3x_Wk", P), ("L3x_Wv", P), ("L3x_Wo", P), ("L3x_bq", 1), ("L3x_bk", 1), ("L3x_bv", 1),
       ("L3x_bo", P), ("L3x_Wqp", P), ("L3x_Wkp", P), ("L3x_bqp", 1), ("L3x_bkp", 1),
       ("L3f_in", NE + 1), ("L3f_w1", NE * P), ("L3f_w2", NE * P), ("L3f_gu", 2 * P), ("L3f_down", P)]
NSTAT = 20 * 256
CONST, NCONST = offsets(CONST_W)
AW, NAW = offsets(A_W)
RAW, NRAW = offsets(RAW_W)
CW, NCW = offsets(C_W)


class Queue:

    def __init__(self, eng, sem):
        self.eng, self.sem, self.n, self.known = eng, sem, 0, {}

    def mark(self, ins):
        self.n += 1
        ins.then_inc(self.sem, 1)
        return self, self.n

    def wait(self, *tokens):
        for t in tokens:
            if t is None:
                continue
            q, n = t
            if self.known.get(q, 0) < n:
                self.eng.wait_ge(q.sem, n)
                self.known[q] = n

    def do(self, after, fn, *a, **k):
        self.wait(*after)
        return self.mark(fn(*a, **k))

    def reset(self):
        self.n, self.known = 0, {}


def bc(ap, axis, n):
    u = ap.unsqueeze(axis)
    shape = list(u.shape)
    shape[axis] = n
    return u.to_broadcast(shape)


def decoder(nc, x, ctx_in, coords, const_d, aw_d, raw_d, intw_d, cw_d, stat_d, out):
    es = ExitStack()
    with es:
        def sb(name, shape, dt=F32):
            return es.enter_context(nc.sbuf_tensor(name, shape, dt))

        X = sb("X", [P, NT, P])
        CT = sb("CT", [P, NTOK])
        CN = sb("CN", [P, NTOK])
        ROT = sb("ROT", [P, 2, NTOK])
        XT = ROT[:, 0, :]
        CC = sb("CC", [P, NCONST])
        WA = sb("WA", [P, NAW])
        WC = sb("WC", [P, NCW])
        L0A = sb("L0A", [P, 4, P])
        L0F = sb("L0F", [P, 9, P])
        L1F = sb("L1F", [P, 9, P])
        G1S = sb("G1S", [P, 256])
        AR = sb("AR", [P, NS, ARENA])
        MASKS = sb("MASKS", [P, 24])
        SM = sb("SM", [P, 64])
        PR5 = sb("PR5", [P, 44])
        PS = [es.enter_context(nc.psum_tensor(f"PS{s}", [P, 4, 512], F32)) for s in range(NS)]

        sems = [es.enter_context(nc.semaphore(f"s_{n}")) for n in ("pe", "act", "dve", "pool")]
        s_load = es.enter_context(nc.semaphore("s_load"))
        s_late = es.enter_context(nc.semaphore("s_late"))
        s_raw = es.enter_context(nc.semaphore("s_raw"))
        s_out = es.enter_context(nc.semaphore("s_out"))
        pe, act, dve, pool = queues = [Queue(e, s) for e, s in zip((nc.tensor, nc.scalar, nc.vector, nc.gpsimd), sems)]
        V, A, G, T = nc.vector, nc.scalar, nc.gpsimd, nc.tensor

        def sync_all():
            nc.all_engine_barrier(sems_to_clear=range(sems[0].num, sems[-1].num + 1))
            for q in queues:
                q.reset()

        def drain_all():
            last = [(q, q.n) for q in queues if q.n]
            for q in queues:
                q.wait(*last)
            nc.sync.wait_ge(sems[2], dve.n)
            sync_all()

        def cc(name):
            o, w = CONST[name]
            return CC[:, o:o + w]

        def wa(name):
            o, w = AW[name]
            return WA[:, o:o + w]

        def wc(name):
            o, w = CW[name]
            return WC[:, o:o + w]

        ident = cc("ident")

        flat = AR[:, :, :].rearrange("p s n -> p (s n)")
        raw = flat[:, 0:NRAW]
        intw = flat[:, NRAW:NRAW + 9 * P].bitcast(I32)
        ctok = flat[:, 4096:4096 + NTOK].rearrange("p (t d) -> p t d", d=P)
        stat = flat[:, 8704:8704 + NSTAT]
        fs = flat[:, 14336:14336 + NT * 3].rearrange("p (t c) -> p t c", c=3)
        assert NRAW + 9 * P <= 4096
        nc.sync.dma_start(ctok, ctx_in.rearrange("(t p) d -> p t d", p=P)).then_inc(s_load, 16)
        nc.sync.dma_start(CC[:, :], const_d).then_inc(s_load, 16)
        nc.sync.dma_start(raw, raw_d).then_inc(s_raw, 16)
        nc.sync.dma_start(intw, intw_d).then_inc(s_raw, 16)
        nc.sync.dma_start(WA[:, :], aw_d).then_inc(s_raw, 16)
        nc.sync.dma_start(X[:, :, :], x.rearrange("(t p) d -> p t d", p=P)).then_inc(s_raw, 16)
        nc.sync.dma_start(fs, coords.rearrange("(t p) c -> p t c", p=P)).then_inc(s_raw, 16)
        nc.sync.dma_start(WC[:, :], cw_d).then_inc(s_late, 16)

        class Stream:
            pass

        streams = []
        for s in range(NS):
            st = Stream()
            st.s = s
            st.ps = PS[s]
            st.x = sb(f"x{s}", [P, TS, P])
            st.xn = sb(f"xn{s}", [P, TS, P])
            st.xb = sb(f"xb{s}", [P, TS, P])
            st.xt = sb(f"xt{s}", [P, ST])
            st.ct = sb(f"ct{s}", [P, ST])
            st.kvt = sb(f"kvt{s}", [P, SQ, KV2])
            st.ot = sb(f"ot{s}", [P, ST])
            st.v2 = sb(f"v2{s}", [P, SQ * GR, 4 * V9])
            st.on = sb(f"on{s}", [P, SQ, P])
            st.bn = sb(f"bn{s}", [P, TS, 6])
            st.mv = sb(f"mv{s}", [P, TS, 2])
            st.sc = sb(f"sc{s}", [P, 640])
            st.ar = AR[:, s, :]
            streams.append(st)

        v = [dve.do([], V.memset, SM[:, :], 0.0)]
        for st in streams:
            pool.do([], G.memset, st.v2[:, :, :], 0.0)
            ones = pool.do([], G.memset, st.on[:, :, :], 0.0)
        for st in streams:
            for g in range(2):
                view = st.v2[64 * g:64 * g + 64, :, :].rearrange("p n (h g k) -> p n h g k", h=2, g=2)
                ones = pool.do([ones], G.memset, view[:, :, :, g, HD], 1.0)
        A.wait_ge(s_load, 32)
        V.wait_ge(s_load, 32)
        T.wait_ge(s_load, 32)
        G.wait_ge(s_load, 32)
        for e in (A, V, T, G):
            e.wait_ge(s_raw, 5 * 16)

        cnt = flat[:, 4096 + NTOK:4096 + 2 * NTOK].rearrange("p (t d) -> p t d", d=P)
        bn6 = sb("bn6", [P, NT, 6])
        mv2 = sb("mv2", [P, NT, 2])
        rstd = sb("rstd", [P, NT])
        for t in range(NT):
            b = dve.do([], V.bn_stats, bn6[:, t, :], ctok[:, t, :])
        dve.wait(b)
        for t in range(NT):
            b = dve.do([], V.bn_aggr, mv2[:, t, :], bn6[:, t, :])
        b = pool.do([b, ones], G.tensor_scalar, rstd[:, :], mv2[:, :, 1], 1e-5, None, ALU.add)
        b = pool.do([b], G.tensor_tensor, rstd[:, :], rstd[:, :], bc(cc("half_neg")[:, 0], 1, NT), ALU.pow)
        for t in range(NT):
            b2 = dve.do([b], V.tensor_scalar, cnt[:, t, :], ctok[:, t, :], mv2[:, t, 0:1], rstd[:, t:t + 1],
                        ALU.subtract, ALU.mult)
        ev = [None, None]
        for k, (src, ready, dst) in enumerate([(ctok, None, CT)] * 4 + [(cnt, b2, CN)] * 4):
            s, t0 = k % 2, 4 * (k % 4)
            pe.wait(ready, ev[s])
            for j in range(4):
                m = T.transpose(PS[s][:, 0, j * P:(j + 1) * P], src[:, t0 + j, :], ident)
            m = pe.mark(m)
            ev[s] = act.do([m], A.copy, dst[:, t0 * P:(t0 + 4) * P], PS[s][:, 0, :])

        w4 = raw[:, 0:4 * P].rearrange("p (w d) -> p w d", d=P)
        sq = flat[:, 14464:14464 + 4 * P].rearrange("p (w d) -> p w d", d=P)
        a = act.do([], A.square, sq, w4)
        a = dve.do([a, v[0]], V.tensor_reduce, SM[:, 0:4], sq, AX, ALU.add)
        a = pool.do([a], G.tensor_scalar, SM[:, 4:8], SM[:, 0:4], 1.0 / P, None, ALU.mult)
        a = pool.do([a], G.tensor_tensor, SM[:, 8:12], SM[:, 4:8], bc(cc("half_pos")[:, 0], 1, 4), ALU.pow)
        a = dve.do([a], V.tensor_scalar, SM[:, 12:16], SM[:, 8:12], 1e-4, None, ALU.add)
        a = dve.do([a], V.reciprocal, SM[:, 16:20], SM[:, 12:16])
        a = dve.do([a], V.tensor_scalar, SM[:, 20:24], SM[:, 16:20], wa("L0a_gain"), float(1 / np.sqrt(P)),
                   ALU.mult, ALU.mult)
        a = dve.do([a], V.tensor_tensor, sq, w4, bc(SM[:, 20:24], 2, P), ALU.mult)
        pe.wait(a)
        for w in range(4):
            m = T.transpose(PS[0][:, 1, w * P:(w + 1) * P], sq[:, w, :], ident)
        m = pe.mark(m)
        act.do([m], A.copy, L0A[:, :, :], PS[0][:, 1, :].rearrange("p (w d) -> p w d", d=P))

        iw = intw.rearrange("p (w d) -> p w d", d=P)
        a = dve.do([], V.tensor_scalar, L0F[:, :, :], iw, float(np.float32(1.0 / 127.0)), None, ALU.mult)
        dve.do([a], V.tensor_scalar, L0F[:, 6:9, :], L0F[:, 6:9, :], 0.5, None, ALU.mult)

        w9 = raw[:, 4 * P:13 * P].rearrange("p (b k) -> p b k", k=32)
        q9 = flat[:, 15104:15104 + 9 * P].rearrange("p (b k) -> p b k", k=32)
        s9 = sb("s9", [P, 36])
        r9 = sb("r9", [P, 36])
        a = dve.do([], V.tensor_reduce, s9[:, :], w9, AX, ALU.max, apply_absolute_value=True)
        a = dve.do([a], V.tensor_scalar, s9[:, :], s9[:, :], float(1 / 7.0), 1e-12, ALU.mult, ALU.max)
        a = dve.do([a], V.reciprocal, r9[:, :], s9[:, :])
        a = dve.do([a], V.tensor_tensor, q9, w9, bc(r9[:, :], 2, 32), ALU.mult)
        a = dve.do([a], V.tensor_scalar, q9, q9, RND, RND, ALU.add, ALU.subtract)
        a = dve.do([a], V.tensor_scalar, q9, q9, -8.0, 7.0, ALU.max, ALU.min)
        a = dve.do([a], V.tensor_tensor, q9, q9, bc(s9[:, :], 2, 32), ALU.mult)
        q9t = flat[:, 15104:15104 + 9 * P].rearrange("p (w d) -> p w d", d=P)
        pe.wait(a)
        for w in range(9):
            m = T.transpose(PS[1][:, 1 + w // 4, (w % 4) * P:(w % 4 + 1) * P], q9t[:, w, :], ident)
        m = pe.mark(m)
        for k in range(3):
            n = min(4, 9 - 4 * k)
            act.do([m], A.copy, L1F[:, 4 * k:4 * k + n, :],
                   PS[1][:, 1 + k, 0:n * P].rearrange("p (w d) -> p w d", d=P))

        th = sb("th", [P, NT, 4])
        nn = sb("nn", [P, NT, 4])
        sc8 = sb("sc8", [P, NT, 8])
        for n in range(4):
            a = dve.do([], V.tensor_scalar, th[:, :, n], fs[:, :, n % 3], float(INV_FREQ[n]), None, ALU.mult)
        a = dve.do([a], V.tensor_scalar, nn[:, :, :], th[:, :, :], float(1 / (2 * np.pi)), RND, ALU.mult, ALU.add)
        a = dve.do([a], V.tensor_scalar, nn[:, :, :], nn[:, :, :], RND, None, ALU.subtract)
        for part in (PI_A, PI_B, PI_C):
            a = dve.do([a], V.scalar_tensor_tensor, th[:, :, :], nn[:, :, :], -part, th[:, :, :], ALU.mult, ALU.add)
        a = dve.do([a], V.tensor_scalar, th[:, :, :], th[:, :, :], -3.1415925, 3.1415925, ALU.max, ALU.min)
        b = act.do([a], A.activation, nn[:, :, :], th[:, :, :], ACT.Abs)
        act.do([a], A.activation, sc8[:, :, 0:4], th[:, :, :], ACT.Sin)
        a = act.do([b], A.activation, sc8[:, :, 4:8], nn[:, :, :], ACT.Sin, scale=-1.0, bias=cc("half_pi"))

        def mask_columns(o, w, name, scaled):
            for k, (bias, scale, mask) in enumerate((("bq", "sq", "parity"), ("bk", "sk", "pair"))):
                for h in range(2):
                    mk = cc(mask)[:, h:h + 1]
                    if scaled:
                        dve.do([], V.tensor_tensor, MASKS[:, o + 4 * k + 2 * h:o + 4 * k + 2 * h + 1], mk,
                               w(f"{name}_{scale}"), ALU.mult)
                    else:
                        dve.do([], V.tensor_copy, MASKS[:, o + 4 * k + 2 * h:o + 4 * k + 2 * h + 1], mk)
                    dve.do([], V.tensor_tensor, MASKS[:, o + 4 * k + 2 * h + 1:o + 4 * k + 2 * h + 2], mk,
                           w(f"{name}_{bias}"), ALU.mult)

        mask_columns(0, wa, "L0x", False)
        mask_columns(8, wa, "L1a", True)
        drain_all()

        def norm(st, ready):
            for j in range(TS):
                a = dve.do([ready], V.bn_stats, st.bn[:, j, :], st.x[:, j, :])
            dve.wait(a)
            for j in range(TS):
                a = dve.do([], V.bn_aggr, st.mv[:, j, :], st.bn[:, j, :])
            a = pool.do([a], G.tensor_scalar, st.sc[:, 0:TS], st.mv[:, :, 1], 1e-5, None, ALU.add)
            a = pool.do([a], G.tensor_tensor, st.sc[:, 2:2 + TS], st.sc[:, 0:TS], cc("half_neg")[:, 0:TS], ALU.pow)
            yield
            for j in range(TS):
                a = dve.do([a], V.tensor_scalar, st.xn[:, j, :], st.x[:, j, :], st.mv[:, j, 0:1],
                           st.sc[:, 2 + j:3 + j], ALU.subtract, ALU.mult)
            pe.wait(a)
            for j in range(TS):
                m = T.transpose(st.ps[:, 0, j * P:(j + 1) * P], st.xn[:, j, :], ident)
            m = pe.mark(m)
            yield
            st.normed = act.do([m], A.copy, st.xt[:, :], st.ps[:, 0, 0:ST])
            yield

        def values(st, src, ready, weight, bank):
            pe.wait(ready)
            w4 = weight.rearrange("p (r g n) -> p r g n", r=GR, g=2)
            for q in range(SQ):
                for g in range(2):
                    m = T.matmul(st.ps[64 * g:64 * g + 64, bank, q * SEQ:(q + 1) * SEQ],
                                 lhsT=src[:, q * SEQ:(q + 1) * SEQ], rhs=w4[:, :, g, :], start=True, stop=True)
            m = pe.mark(m)
            for g in range(2):
                rows = slice(64 * g, 64 * g + 64)
                src_v = st.ps[rows, bank, 0:SQ * SEQ].rearrange("p (n h d) -> p n h d", h=2, d=HD)
                dst_v = st.v2[rows, :, :].rearrange("p n (h g k) -> p n h g k", h=2, g=2)[:, :, :, g, 0:HD]
                t = act.do([m], A.copy, dst_v, src_v)
            return t

        def softmax(st, n, width, E, mx, scale):
            sc3 = st.ps[:, :, :].rearrange("p r (a k) -> p (r a) k", k=width)
            e3 = E.rearrange("p (n k) -> p n k", k=width)
            a = dve.do([n], V.tensor_reduce, mx, sc3, AX, ALU.max)
            s = dve.do([a], V.tensor_tensor, e3, sc3, bc(mx, 2, width), ALU.subtract)
            e = act.do([s], A.activation, E, E, ACT.Exp, scale=scale)
            return s, e

        def weigh(st, AT, ready, v_ready, eps):
            pe.wait(ready, v_ready)
            for q in range(SQ):
                for r in range(GR):
                    o = ((q % 2) * GR + r) * 4 * V9
                    m = T.matmul(st.ps[:, q // 2, o:o + 4 * V9], lhsT=AT[:, (r * SQ + q) * P:(r * SQ + q + 1) * P],
                                 rhs=st.v2[:, q * GR + r, :], start=True, stop=True)
            m = pe.mark(m)
            yield
            rec = st.sc[:, 256:320].rearrange("p (b n c) -> p b n c", b=2, c=4)
            for b in range(2):
                o5 = st.ps[:, b, 0:8 * 4 * V9].rearrange("p (n c k) -> p n c k", c=4, k=V9)
                if eps:
                    a = dve.do([m], V.tensor_scalar, rec[:, b, :, :], o5[:, :, :, HD], eps, None, ALU.add)
                    a = dve.do([a], V.reciprocal, rec[:, b, :, :], rec[:, b, :, :])
                else:
                    a = dve.do([m], V.reciprocal, rec[:, b, :, :], o5[:, :, :, HD])
            for b in range(2):
                for h in range(2):
                    rows = slice(64 * h, 64 * h + 64)
                    o5 = st.ps[rows, b, 0:8 * 4 * V9].rearrange("p (n h g k) -> p n h g k", h=2, g=2, k=V9)
                    dst = st.on[rows, :, :].rearrange("p q (r g h d) -> p (q r) g h d", r=GR, g=2, h=2)
                    r4 = rec[rows, b, :, :].rearrange("p n (h g) -> p n h g", h=2)[:, :, h, :]
                    a = dve.do([a], V.tensor_tensor, dst[:, 8 * b:8 * b + 8, :, h, :], o5[:, :, h, :, 0:HD],
                               bc(r4, 3, HD), ALU.mult)
            st.weighed = a
            yield

        def project_out(st, weight, scale_v, bias_v, scale_o, res):
            pe.wait(st.weighed)
            for q in range(SQ):
                m = T.matmul(st.ps[:, 2, q * SEQ:(q + 1) * SEQ], lhsT=st.on[:, q, :], rhs=cc("fold"),
                             start=True, stop=True)
            m = pe.mark(m)
            if bias_v is None:
                a = act.do([m], A.copy, st.ot[:, :], st.ps[:, 2, 0:ST])
            else:
                a = act.do([m], A.activation, st.ot[:, :], st.ps[:, 2, 0:ST], ACT.Identity, scale=scale_v,
                           bias=bias_v)
            yield
            pe.wait(a)
            for j in range(TS):
                m = T.matmul(st.ps[:, 3, j * P:(j + 1) * P], lhsT=st.ot[:, j * P:(j + 1) * P], rhs=weight,
                             start=True, stop=True)
            m = pe.mark(m)
            y = st.ps[:, 3, 0:ST].rearrange("p (j d) -> p j d", d=P)
            st.done = dve.do([m, res[1]], V.scalar_tensor_tensor, st.x[:, :, :], y, scale_o, res[0],
                             ALU.mult, ALU.add)
            yield

        def attention(st, name, w, src, masks=None, mix=None, rope=None, scale_v=1.0, scale_o=1.0):
            yield from norm(st, st.done)
            ps, ar = st.ps, st.ar
            xb = pool.do([st.done], G.tensor_tensor, st.xb[:, :, :], st.x[:, :, :], bc(w(f"{name}_bo"), 1, TS), ALU.add)
            n = [("Wq", st.xt, 0, 0), ("Wk", src, 2, 0)]
            if rope:
                n += [("Wqp", st.xt, 0, ST), ("Wkp", src, 2, ST)]
            pe.wait(st.normed, st.ct_ready)
            for wn, s_, bank, o in n:
                m = T.matmul(ps[:, bank, o:o + ST], lhsT=w(f"{name}_{wn}"), rhs=s_[:, :], start=True, stop=True)
            m = pe.mark(m)
            v_ready = values(st, src, st.normed, w(f"{name}_Wv"), 1)
            yield
            E, AT = ar[:, 4096:6144], ar[:, 6144:8192]
            mx = st.sc[:, 64:96]
            if mix is None:
                qm = ar[:, 0:2 * ST].rearrange("p (q h t) -> p q h t", q=SQ, h=2)
                km = ar[:, 2 * ST:4 * ST].rearrange("p (q h t) -> p q h t", q=SQ, h=2)
                if rope:
                    cs, r = rope
                    rq = ar[:, 4 * ST:8 * ST].rearrange("p (c n t) -> p c n t", c=2, n=2)
                    for c, biases in enumerate((("bq", "bk"), ("bqp", "bkp"))):
                        for k, bias in enumerate(biases):
                            a = dve.do([m, r], V.scalar_tensor_tensor, rq[:, c, k, :], ps[:, 2 * k, c * ST:(c + 1) * ST],
                                       w(f"{name}_{bias}"), cs[:, c, :], ALU.add, ALU.mult)
                    a = dve.do([a], V.tensor_tensor, rq[:, 0, :, :], rq[:, 0, :, :], rq[:, 1, :, :], ALU.add)
                    evs = []
                    for k, dst in enumerate((qm, km)):
                        for h in range(2):
                            mk = cc(("parity", "pair")[k])[:, h:h + 1]
                            src3 = rq[:, 0, k, :].rearrange("p (q t) -> p q t", q=SQ)
                            if h == 0:
                                evs.append(dve.do([a], V.tensor_scalar, dst[:, :, h, :], src3, mk, None, ALU.mult))
                            else:
                                evs.append(pool.do([a], G.tensor_scalar, dst[:, :, h, :], src3, mk, None, ALU.mult))
                else:
                    evs = []
                    for k, dst in enumerate((qm, km)):
                        for h in range(2):
                            o = masks + 4 * k + 2 * h
                            src3 = ps[:, 2 * k, 0:ST].rearrange("p (q t) -> p q t", q=SQ)
                            if k == 0:
                                evs.append(dve.do([m], V.tensor_scalar, dst[:, :, h, :], src3, MASKS[:, o:o + 1],
                                                  MASKS[:, o + 1:o + 2], ALU.mult, ALU.add))
                            else:
                                evs.append(act.do([m], A.activation, dst[:, :, h, :], src3, ACT.Identity,
                                                  scale=MASKS[:, o:o + 1], bias=MASKS[:, o + 1:o + 2]))
                yield
                pe.wait(v_ready, *evs)
                for q in range(SQ):
                    for r in range(GR):
                        rows = slice(32 * r, 32 * r + 32)
                        m = T.matmul(ps[:, r, q * P:(q + 1) * P], lhsT=qm[rows, q, :, :], rhs=km[rows, q, :, :],
                                     start=True, stop=True)
                m = pe.mark(m)
            else:
                qf, kf = E[:, 0:ST], E[:, ST:2 * ST]
                a = dve.do([m], V.tensor_scalar, qf, ps[:, 0, 0:ST], w(f"{name}_bq"), None, ALU.add)
                b = act.do([m], A.activation, kf, ps[:, 2, 0:ST], ACT.Identity, bias=w(f"{name}_bk"))
                qp = ar[:, 0:16 * ST].rearrange("p (q g t) -> p q g t", q=SQ, g=H)
                q3 = qf.rearrange("p (q t) -> p q t", q=SQ)
                ts = [None] * 3
                for g in range(H):
                    if g % 8 < 3:
                        ts[0] = pool.do([a], G.tensor_scalar, qp[:, :, g, :], q3, mix[:, g:g + 1], None, ALU.mult)
                    elif g % 8 < 6:
                        ts[1] = dve.do([a], V.tensor_scalar, qp[:, :, g, :], q3, mix[:, g:g + 1], None, ALU.mult)
                    else:
                        ts[2] = act.do([a], A.activation, qp[:, :, g, :], q3, ACT.Copy, scale=mix[:, g:g + 1])
                yield
                pe.wait(v_ready, b, *ts)
                for q in range(SQ):
                    for g in range(H // 2):
                        o = q * P + (g % 2) * SEQ
                        m = T.matmul(ps[:, g // 2, o:o + SEQ], lhsT=qp[:, q, 2 * g:2 * g + 2, :],
                                     rhs=kf[:, q * SEQ:(q + 1) * SEQ], start=True, stop=True)
                m = pe.mark(m)
            yield
            s, e = softmax(st, m, SEQ, E, mx, float(1 / np.sqrt(np.float32(HD))))
            yield
            pe.wait(s, e)
            for n in range(SQ * GR):
                m = T.transpose(ps[:, n // 4, (n % 4) * P:(n % 4 + 1) * P], E[:, n * P:(n + 1) * P], ident)
            m = pe.mark(m)
            yield
            p2 = ps[:, :, :].rearrange("p r n -> p (r n)")
            c1 = act.do([m], A.copy, AT[:, 0:1024], p2[:, 0:1024])
            c2 = dve.do([m], V.tensor_copy, AT[:, 1024:2048], p2[:, 1024:2048])
            yield
            pe.wait(c1)
            yield from weigh(st, AT, c2, v_ready, None)
            yield from project_out(st, w(f"{name}_Wo"), scale_v, w(f"{name}_bv"), scale_o, (st.xb[:, :, :], xb))

        def l0_attention(st):
            yield from norm(st, st.done)
            ps, ar = st.ps, st.ar
            pe.wait(st.normed)
            w = L0A[:, :, :].rearrange("p w d -> p (w d)")
            for j in range(TS):
                T.matmul(ps[:, j, 0:2 * P], lhsT=st.xt[:, j * P:(j + 1) * P], rhs=w[:, 0:2 * P], start=True, stop=True)
            m = T.matmul(ps[:, 2, 0:ST], lhsT=w[:, 2 * P:3 * P], rhs=st.xt[:, :], start=True, stop=True)
            m = pe.mark(m)
            yield
            qk = ar[:, 0:512].rearrange("p (j n d) -> p j n d", j=TS, d=HD)
            sq = ar[:, 512:1024].rearrange("p (j n d) -> p j n d", j=TS, d=HD)
            vt = ar[:, 1024:1024 + ST]
            pq = ps[:, 0:TS, 0:2 * P].rearrange("p j (n d) -> p j n d", d=HD)
            a = act.do([m], A.square, sq, pq)
            vt_ready = act.do([m], A.copy, vt, ps[:, 2, 0:ST])
            ss = st.sc[:, 64:128].rearrange("p (j n) -> p j n", j=TS)
            a = dve.do([a], V.tensor_reduce, ss, sq, AX, ALU.add)
            a = pool.do([a], G.tensor_scalar, ss, ss, 1.0 / HD, None, ALU.mult)
            a = pool.do([a], G.tensor_tensor, ss, ss, bc(bc(cc("half_pos")[:, 0], 1, 2 * H), 1, TS), ALU.pow)
            yield
            a = dve.do([a], V.tensor_scalar, ss, ss, 1e-4, None, ALU.add)
            a = dve.do([a], V.reciprocal, ss, ss)
            a = dve.do([a], V.tensor_tensor, qk, pq, bc(ss, 3, HD), ALU.mult)
            qf = ar[:, 0:512].rearrange("p (j n) -> p j n", j=TS)
            pe.wait(a)
            for q in range(SQ):
                rows = slice(SEQ * (q % 2), SEQ * (q % 2) + SEQ)
                m = T.matmul(ps[:, q % 2, (q // 2) * P:(q // 2 + 1) * P], lhsT=qf[rows, q // 2, 0:P],
                             rhs=qf[rows, q // 2, P:2 * P], start=True, stop=True)
            m = pe.mark(m)
            yield
            g4 = ar[:, 1536:2048].rearrange("p (a b n) -> p a b n", a=2, b=2)
            mx = st.sc[:, 128:132].rearrange("p (a b) -> p a b", a=2)
            a = dve.do([m], V.tensor_tensor, g4, ps[:, 0:2, 0:2 * P].rearrange("p a (b n) -> p a b n", b=2),
                       bc(bc(cc("head_bias"), 1, 2), 1, 2), ALU.add)
            a = dve.do([a], V.tensor_reduce, mx, g4, AX, ALU.max)
            a = dve.do([a], V.tensor_tensor, g4, g4, bc(mx, 3, P), ALU.subtract)
            a = act.do([a], A.activation, g4, g4, ACT.Exp, scale=0.125)
            a = dve.do([a], V.tensor_reduce, mx, g4, AX, ALU.add)
            a = dve.do([a], V.reciprocal, mx, mx)
            a = dve.do([a], V.tensor_tensor, g4, g4, bc(mx, 3, P), ALU.mult)
            yield
            pe.wait(a)
            for q in range(SQ):
                m = T.matmul(ps[:, 3, q * P:(q + 1) * P], lhsT=g4[:, q % 2, q // 2, :], rhs=w[:, 3 * P:4 * P],
                             start=True, stop=True)
            m = pe.mark(m)
            mm = ar[:, 2048:2560]
            a = act.do([m], A.copy, mm, ps[:, 3, :])
            yield
            pe.wait(a, vt_ready)
            for q in range(SQ):
                rows = slice(SEQ * (q % 2), SEQ * (q % 2) + SEQ)
                m = T.matmul(ps[rows, 2, (q // 2) * P:(q // 2 + 1) * P], lhsT=vt[:, q * SEQ:(q + 1) * SEQ],
                             rhs=mm[:, q * P:(q + 1) * P], start=True, stop=True)
            m = pe.mark(m)
            a = dve.do([m], V.tensor_tensor, st.xn[:, :, :], st.xn[:, :, :],
                       ps[:, 2, 0:ST].rearrange("p (j d) -> p j d", d=P), ALU.add)
            st.done = dve.do([a], V.scalar_tensor_tensor, st.x[:, :, :], st.xn[:, :, :], float(0.5 / np.sqrt(0.5)),
                             st.x[:, :, :], ALU.mult, ALU.add)
            yield

        def l0_ffn(st):
            yield from norm(st, st.done)
            ps, ar = st.ps, st.ar
            pe.wait(st.normed)
            for k in range(6):
                b, o = (k // 3) * 2 + (k % 3) // 2, ((k % 3) % 2) * ST
                m = T.matmul(ps[:, b, o:o + ST], lhsT=L0F[:, k, :], rhs=st.xt[:, :], start=True, stop=True)
            m = pe.mark(m)
            yield
            gate = ps[:, 0:2, :].rearrange("p b n -> p (b n)")[:, 0:3 * ST]
            up = ps[:, 2:4, :].rearrange("p b n -> p (b n)")[:, 0:3 * ST]
            t1, h = ar[:, 0:3 * ST], ar[:, 3 * ST:6 * ST]
            a = act.do([m], A.activation, t1, gate, ACT.Tanh, scale=0.5)
            a = dve.do([a], V.scalar_tensor_tensor, h, t1, 1.0, gate, ALU.add, ALU.mult)
            a = dve.do([a], V.tensor_tensor, h, h, up, ALU.mult)
            yield
            pe.wait(a)
            for j in range(TS):
                for k in range(3):
                    m = T.matmul(ps[:, 0, j * P:(j + 1) * P], lhsT=h[:, k * ST + j * P:k * ST + (j + 1) * P],
                                 rhs=L0F[:, 6 + k, :], start=(k == 0), stop=(k == 2))
            m = pe.mark(m)
            st.done = dve.do([m], V.tensor_tensor, st.x[:, :, :], st.x[:, :, :],
                             ps[:, 0, 0:ST].rearrange("p (j d) -> p j d", d=P), ALU.add)
            yield

        def l2_attention(st):
            yield from norm(st, st.done)
            ps, ar = st.ps, st.ar
            w = wc("L2a_w")
            pe.wait(st.normed)
            for k in range(2):
                m = T.matmul(ps[:, 0, k * ST:(k + 1) * ST], lhsT=w[:, k * P:(k + 1) * P], rhs=st.xt[:, :],
                             start=True, stop=True)
            m = pe.mark(m)
            v_ready = values(st, st.xt, st.normed, w[:, 2 * P:3 * P], 1)
            yield
            qk = ps[:, 0, :]
            lo, f = ar[:, 0:512], ar[:, 512:1024]
            a = dve.do([m], V.tensor_scalar, lo, qk, 0.0, None, ALU.min)
            a = act.do([a], A.activation, lo, lo, ACT.Exp)
            a = dve.do([a], V.scalar_tensor_tensor, f, qk, 0.0, lo, ALU.max, ALU.add)
            dst = ar[:, 1024:2048].rearrange("p (k q h t) -> p k q h t", k=2, q=SQ, h=2)
            evs = []
            for k in range(2):
                for h in range(2):
                    eng, on = ((dve, V), (pool, G))[k]
                    mk = cc(("parity", "pair")[k])[:, h:h + 1]
                    evs.append(eng.do([a], on.tensor_scalar, dst[:, k, :, h, :],
                                      f[:, k * ST:(k + 1) * ST].rearrange("p (q t) -> p q t", q=SQ), mk, None, ALU.mult))
            yield
            pe.wait(v_ready, *evs)
            for q in range(SQ):
                for r in range(GR):
                    rows = slice(32 * r, 32 * r + 32)
                    m = T.matmul(ps[:, r, q * P:(q + 1) * P], lhsT=dst[rows, 1, q, :, :], rhs=dst[rows, 0, q, :, :],
                                 start=True, stop=True)
            m = pe.mark(m)
            AT = ar[:, 6144:8192]
            a = dve.do([m], V.tensor_tensor, AT.rearrange("p (n k) -> p n k", k=P),
                       ps[:, :, :].rearrange("p r (q k) -> p (r q) k", k=P), bc(cc("causal"), 1, GR * SQ), ALU.mult)
            yield
            yield from weigh(st, AT, a, v_ready, 1e-6)
            yield from project_out(st, wc("L2a_Wo"), 1.0, None, 1.0, (st.x[:, :, :], st.done))

        def l2_cross(st):
            yield from norm(st, st.done)
            ps, ar = st.ps, st.ar
            for j in range(TS):
                a = dve.do([st.normed], V.bn_stats, st.bn[:, j, :], st.xn[:, j, :])
            dve.wait(a)
            for j in range(TS):
                a = dve.do([], V.bn_aggr, st.mv[:, j, :], st.bn[:, j, :])
            a = pool.do([a], G.tensor_scalar, st.sc[:, 0:TS], st.mv[:, :, 1], 1e-5, None, ALU.add)
            a = pool.do([a], G.tensor_tensor, st.sc[:, 2:2 + TS], st.sc[:, 0:TS], cc("half_neg")[:, 0:TS], ALU.pow)
            qB = ar[:, 0:2048].rearrange("p (c q h t) -> p c q h t", c=8, q=2, h=2)
            kB = ar[:, 2048:4096].rearrange("p (c n) -> p c n", c=8)
            vB = ar[:, 4096:4096 + 2 * H2 * (D2 + 1)].rearrange("p (q n) -> p q n", q=2)
            E = ar[:, 6400:8448]
            AT = ar[:, 2048:4096]
            z1 = pool.do([st.done], G.memset, ar[:, 0:2048], 0.0)
            z2 = pool.do([], G.memset, vB.rearrange("p q (h k) -> p (q h) k", k=D2 + 1)[:, :, D2], 1.0)
            yield
            for j in range(TS):
                a = dve.do([a], V.tensor_scalar, st.xn[:, j, :], st.xn[:, j, :], st.mv[:, j, 0:1],
                           st.sc[:, 2 + j:3 + j], ALU.subtract, ALU.mult)
            pe.wait(a)
            for j in range(TS):
                m = T.transpose(ps[:, 0, j * P:(j + 1) * P], st.xn[:, j, :], ident)
            m = pe.mark(m)
            kv_ready = act.do([m, st.cn_ready], A.activation, st.kvt[:, :, SEQ:KV2],
                              ps[:, 0, 0:ST].rearrange("p (q t) -> p q t", q=SQ), ACT.Identity,
                              scale=wc("L2x_lg"), bias=wc("L2x_lb"))
            yield
            free = kv_ready
            for half in range(TS):
                q0 = 2 * half
                kvt = st.kvt[:, q0:q0 + 2, :]
                pe.wait(kv_ready, free)
                for c in range(8):
                    m = T.matmul(ps[:, c // 4, (c % 4) * P:(c % 4 + 1) * P], lhsT=wc("L2x_Wq")[:, c * P:(c + 1) * P],
                                 rhs=kvt[:, :, SEQ:KV2], start=True, stop=True)
                m = pe.mark(m)
                for h in range(2):
                    rows = slice(64 * h, 64 * h + 64)
                    src = ps[rows, 0:2, :].rearrange("p b (n t) -> p (b n) t", t=SEQ)
                    dst = qB[rows, :, :, :, :].rearrange("p c q h t -> p (c q) h t")[:, :, h, :]
                    q_ready = dve.do([m, z1], V.tensor_copy, dst, src)
                yield
                for q in range(2):
                    b0 = 2 - 2 * q
                    pe.wait(q_ready)
                    for n in range(2):
                        m = T.matmul(ps[:, b0 + n, :], lhsT=kvt[:, q, :],
                                     rhs=wc("L2x_Wkv")[:, 1024 + 512 * n:1536 + 512 * n], start=True, stop=True)
                    m = pe.mark(m)
                    src = ps[:, b0:b0 + 2, :].rearrange("p b (n d) -> p (b n) d", d=D2)
                    dst = vB[:, q, :].rearrange("p (h k) -> p h k", k=D2 + 1)[:, :, 0:D2]
                    v_ready = act.do([m, z2], A.copy, dst, src)
                    yield
                pe.wait(v_ready)
                for c in range(8):
                    m = T.matmul(ps[:, c // 2, (c % 2) * 256:(c % 2) * 256 + 256], lhsT=wc("L2x_Wkv")[:, c * P:(c + 1) * P],
                                 rhs=kvt, start=True, stop=True)
                m = pe.mark(m)
                p2 = ps[:, :, :].rearrange("p b n -> p (b n)")
                kf = ar[:, 2048:4096]
                k1 = act.do([m], A.copy, kf[:, 0:1024], p2[:, 0:1024])
                k2 = dve.do([m], V.tensor_copy, kf[:, 1024:2048], p2[:, 1024:2048])
                yield
                pe.wait(k1, k2)
                for q in range(2):
                    for c in range(8):
                        m = T.matmul(ps[:, 2 * q + c // 4, (c % 4) * P:(c % 4 + 1) * P], lhsT=qB[:, c, q, :, :],
                                     rhs=kB[:, c, q * KV2:(q + 1) * KV2], start=True, stop=True)
                m = pe.mark(m)
                yield
                s, e = softmax(st, m, KV2, E, st.sc[:, 64:80], D2 ** -0.5)
                yield
                pe.wait(s, e)
                for n in range(16):
                    m = T.transpose(ps[:, n // 4, (n % 4) * P:(n % 4 + 1) * P], E[:, n * P:(n + 1) * P], ident)
                m = pe.mark(m)
                c1 = act.do([m], A.copy, AT[:, 0:1024], p2[:, 0:1024])
                c2 = dve.do([m], V.tensor_copy, AT[:, 1024:2048], p2[:, 1024:2048])
                yield
                pe.wait(c1, c2)
                for q in range(2):
                    for h in range(H2):
                        o = (q * 8 + h // 2) * P + (h % 2) * 64
                        b, n = h // 7, (h % 7) * (D2 + 1)
                        m = T.matmul(ps[64 * q:64 * q + 64, b, n:n + D2 + 1], lhsT=AT[:, o:o + 64],
                                     rhs=vB[:, q, h * (D2 + 1):(h + 1) * (D2 + 1)], start=True, stop=True)
                m = pe.mark(m)
                yield
                O, OT = E[:, 0:1024], E[:, 1024:2048]
                rec = st.sc[:, 96:112]
                for b in range(3):
                    n = min(7, H2 - 7 * b)
                    o3 = ps[:, b, 0:n * (D2 + 1)].rearrange("p (h k) -> p h k", k=D2 + 1)
                    a = dve.do([m], V.reciprocal, rec[:, 7 * b:7 * b + n], o3[:, :, D2])
                for b in range(3):
                    n = min(7, H2 - 7 * b)
                    o3 = ps[:, b, 0:n * (D2 + 1)].rearrange("p (h k) -> p h k", k=D2 + 1)
                    a2 = dve.do([a], V.tensor_tensor, O[:, 448 * b:448 * b + 64 * n].rearrange("p (h d) -> p h d", d=D2),
                                o3[:, :, 0:D2], bc(rec[:, 7 * b:7 * b + n], 2, D2), ALU.mult)
                yield
                pe.wait(a2)
                for c in range(8):
                    m = T.transpose(ps[:, c // 4, (c % 4) * P:(c % 4 + 1) * P], O[:, c * P:(c + 1) * P], ident)
                m = pe.mark(m)
                a = act.do([m], A.copy, OT, p2[:, 0:1024])
                yield
                pe.wait(a)
                for c in range(8):
                    m = T.matmul(ps[:, 3, 0:P], lhsT=OT[:, c * P:(c + 1) * P],
                                 rhs=wc("L2x_Wo")[:, c * P:(c + 1) * P], start=(c == 0), stop=(c == 7))
                m = pe.mark(m)
                free = st.done = dve.do([m], V.tensor_tensor, st.x[:, half, :], st.x[:, half, :], ps[:, 3, 0:P], ALU.add)
                yield

        def ranks(st, lg, ready, ties, gt, cnt):
            le = bc(lg, 3, NE)
            lj = bc(lg, 2, NE)
            a = dve.do([ready], V.tensor_tensor, gt, lj, le, ALU.is_gt)
            if ties is not None:
                b = dve.do([ready], V.tensor_tensor, ties, lj, le, ALU.is_equal)
                b = dve.do([b], V.tensor_tensor, ties, ties,
                           bc(cc("before").rearrange("p (e j) -> p e j", e=NE), 1, TS), ALU.mult)
                a = dve.do([a, b], V.tensor_tensor, gt, gt, ties, ALU.add)
            return dve.do([a], V.tensor_reduce, cnt, gt, AX, ALU.add)

        def l2_ffn(st):
            yield from norm(st, st.done)
            ps, ar, sc = st.ps, st.ar, st.sc
            xb = pool.do([st.done], G.tensor_tensor, st.xb[:, :, :], st.x[:, :, :], bc(wc("L2f_bb"), 1, TS), ALU.add)
            pe.wait(st.normed)
            N = P + NE
            for j in range(TS):
                m = T.matmul(ps[:, 1, j * 256:j * 256 + N], lhsT=st.xt[:, j * P:(j + 1) * P], rhs=wc("L2f_in"),
                             start=True, stop=True)
            m = pe.mark(m)
            yield
            p3 = ps[:, 1, :].rearrange("p (j n) -> p j n", j=TS)
            lg = sc[:, 8:24].rearrange("p (j e) -> p j e", j=TS)
            gt = sc[:, 128:256].rearrange("p (j e k) -> p j e k", j=TS, e=NE)
            cnt = sc[:, 24:40].rearrange("p (j e) -> p j e", j=TS)
            mx = sc[:, 4:6]
            ready = dve.do([m], V.tensor_tensor, lg, p3[:, :, P:N], bc(wc("L2f_rb"), 1, TS), ALU.add)
            c = ranks(st, lg, ready, None, gt, cnt)
            a = dve.do([ready], V.tensor_reduce, mx, lg, AX, ALU.max)
            a = dve.do([a, c], V.tensor_tensor, lg, lg, bc(mx, 2, NE), ALU.subtract)
            a = act.do([a], A.activation, lg, lg, ACT.Exp)
            c = dve.do([c], V.tensor_scalar, cnt, cnt, 1.5, None, ALU.is_lt)
            a = dve.do([a, c], V.tensor_tensor, lg, lg, cnt, ALU.mult)
            a = dve.do([a], V.tensor_reduce, mx, lg, AX, ALU.add)
            a = dve.do([a], V.reciprocal, mx, mx)
            a = dve.do([a], V.tensor_scalar, mx, mx, 2.0, None, ALU.mult)
            a = dve.do([a], V.tensor_tensor, lg, lg, bc(mx, 2, NE), ALU.mult)
            yield
            ws = ar[:, 0:ST].rearrange("p (j n) -> p j n", j=TS)
            for j in range(TS):
                a2 = dve.do([a], V.tensor_tensor, ws[:, j, :].rearrange("p (e r) -> p e r", e=NE),
                            p3[:, j, 0:P].rearrange("p (e r) -> p e r", e=NE), bc(lg[:, j, :], 2, P // NE), ALU.mult)
            pe.wait(a2)
            for j in range(TS):
                m = T.transpose(ps[:, 0, j * P:(j + 1) * P], ws[:, j, :], ident)
            m = pe.mark(m)
            wt = ar[:, ST:2 * ST]
            a = act.do([m], A.copy, wt, ps[:, 0, 0:ST])
            yield
            pe.wait(a)
            for j in range(TS):
                T.matmul(ps[:, 2, j * P:(j + 1) * P], lhsT=st.xt[:, j * P:(j + 1) * P], rhs=wc("L2f_base"),
                         start=True, stop=False)
                m = T.matmul(ps[:, 2, j * P:(j + 1) * P], lhsT=wt[:, j * P:(j + 1) * P], rhs=wc("L2f_B"),
                             start=False, stop=True)
            m = pe.mark(m)
            st.done = dve.do([m, xb], V.tensor_tensor, st.x[:, :, :], st.xb[:, :, :],
                             ps[:, 2, 0:ST].rearrange("p (j d) -> p j d", d=P), ALU.add)
            yield

        def l3_ffn(st):
            yield from norm(st, st.done)
            ps, ar, sc = st.ps, st.ar, st.sc
            pe.wait(st.normed)
            for j in range(TS):
                m = T.matmul(ps[:, 3, j * 256:j * 256 + NE + 1], lhsT=st.xt[:, j * P:(j + 1) * P], rhs=wc("L3f_in"),
                             start=True, stop=True)
            mr = pe.mark(m)
            for n in range(2):
                m = T.matmul(ps[:, 2, n * ST:(n + 1) * ST], lhsT=wc("L3f_gu")[:, n * P:(n + 1) * P], rhs=st.xt[:, :],
                             start=True, stop=True)
            ms = pe.mark(m)
            yield
            p3 = ps[:, 3, :].rearrange("p (j n) -> p j n", j=TS)
            lg = sc[:, 8:24].rearrange("p (j e) -> p j e", j=TS)
            gt = sc[:, 128:256].rearrange("p (j e k) -> p j e k", j=TS, e=NE)
            eq = sc[:, 320:448].rearrange("p (j e k) -> p j e k", j=TS, e=NE)
            cnt = sc[:, 24:40].rearrange("p (j e) -> p j e", j=TS)
            mx = sc[:, 4:6]
            sg = sc[:, 40:42]
            b = act.do([mr], A.activation, sg, p3[:, :, NE], ACT.Tanh, scale=0.5)
            a = b
            b = dve.do([b], V.tensor_scalar, sg, sg, 1.0, 0.25, ALU.add, ALU.mult)
            a = dve.do([a], V.tensor_reduce, mx, p3[:, :, 0:NE], AX, ALU.max)
            a = dve.do([a], V.tensor_tensor, lg, p3[:, :, 0:NE], bc(mx, 2, NE), ALU.subtract)
            a = act.do([a], A.activation, lg, lg, ACT.Exp)
            a = dve.do([a], V.tensor_reduce, mx, lg, AX, ALU.add)
            a = dve.do([a], V.reciprocal, mx, mx)
            a = dve.do([a], V.tensor_tensor, lg, lg, bc(mx, 2, NE), ALU.mult)
            c = ranks(st, lg, a, eq, gt, cnt)
            c = dve.do([c], V.tensor_scalar, cnt, cnt, 1.5, 0.5, ALU.is_lt, ALU.mult)
            c = dve.do([c], V.tensor_tensor, lg, lg, cnt, ALU.mult)
            th, hs = ar[:, 0:ST], ar[:, ST:2 * ST]
            a = act.do([ms], A.activation, th, ps[:, 2, 0:ST], ACT.Tanh, scale=0.5)
            a = dve.do([a], V.scalar_tensor_tensor, hs, th, 1.0, ps[:, 2, 0:ST], ALU.add, ALU.mult)
            hs_ready = dve.do([a], V.tensor_tensor, hs, hs, ps[:, 2, ST:2 * ST], ALU.mult)
            yield
            acc = st.x
            last = None
            for n in range(2):
                pe.wait(last, b)
                for e in range(4):
                    m = T.matmul(ps[:, e // 2, (e % 2) * ST:(e % 2 + 1) * ST],
                                 lhsT=wc("L3f_w1")[:, (4 * n + e) * P:(4 * n + e + 1) * P], rhs=st.xt[:, :],
                                 start=True, stop=True)
                m = pe.mark(m)
                he, t4 = ar[:, 1024:2048], ar[:, 2048:3072]
                pg = ps[:, 0:2, :].rearrange("p b n -> p (b n)")
                a = act.do([m], A.activation, t4, pg, ACT.Tanh, scale=0.5)
                a = dve.do([a], V.scalar_tensor_tensor, he, t4, 1.0, pg, ALU.add, ALU.mult)
                yield
                pe.wait(a, c, hs_ready)
                for j in range(TS):
                    for e in range(4):
                        m = T.matmul(ps[:, 2 + j, e * P:(e + 1) * P], lhsT=he[:, e * ST + j * P:e * ST + (j + 1) * P],
                                     rhs=wc("L3f_w2")[:, (4 * n + e) * P:(4 * n + e + 1) * P], start=True, stop=True)
                    if n == 0:
                        m = T.matmul(ps[:, j, 0:P], lhsT=hs[:, j * P:(j + 1) * P], rhs=wc("L3f_down"),
                                     start=True, stop=True)
                m = pe.mark(m)
                yield
                for e in range(4):
                    for j in range(TS):
                        k = lg[:, j, 4 * n + e:4 * n + e + 1]
                        last_j = dve.do([m, last], V.scalar_tensor_tensor, acc[:, j, :], ps[:, 2 + j, e * P:(e + 1) * P],
                                        k, acc[:, j, :], ALU.mult, ALU.add)
                    last = last_j
                if n == 0:
                    for j in range(TS):
                        last_j = dve.do([last], V.scalar_tensor_tensor, acc[:, j, :], ps[:, j, 0:P], sg[:, j:j + 1],
                                        acc[:, j, :], ALU.mult, ALU.add)
                    last = last_j
                yield
            st.done = last

        def l3_attention(st):
            yield from norm(st, st.done)
            ps, ar, sc = st.ps, st.ar, st.sc
            w = wc("L3a_w")
            pe.wait(st.normed)
            for k in range(3):
                m = T.matmul(ps[:, k // 2, (k % 2) * ST:(k % 2 + 1) * ST], lhsT=w[:, k * P:(k + 1) * P], rhs=st.xt[:, :],
                             start=True, stop=True)
            for j in range(TS):
                m = T.matmul(ps[:, 2, j * 4:j * 4 + 4], lhsT=st.xt[:, j * P:(j + 1) * P], rhs=wc("L3a_Wb"),
                             start=True, stop=True)
            m = pe.mark(m)
            s3 = ar[:, 0:768]
            fir = ar[:, 768:1536]
            paths = ar[:, 1536:2816].rearrange("p (j c n) -> p j c n", j=TS, c=5)
            bv = ar[:, 2816:3072].rearrange("p (j n) -> p j n", j=TS)
            D0 = 3072
            cb = ar[:, D0:D0 + 804].rearrange("p (n t) -> p n t", t=SEQ + 3)
            acc = ar[:, D0 + 804:D0 + 1572]
            th = ar[:, D0 + 1572:D0 + 2340]
            vp = ar[:, D0 + 2340:D0 + 2340 + SQ * 127].rearrange("p (q t) -> p q t", q=SQ)
            z = pool.do([st.done], G.memset, cb[:, :, 0:3], 0.0)
            z2 = pool.do([], G.memset, vp[:, :, 0:63], 0.0)
            yield
            beta = sc[:, 8:16].rearrange("p (h j) -> p h j", j=TS)
            b = act.do([m], A.activation, beta.rearrange("p h j -> p j h"),
                       ps[:, 2, 0:8].rearrange("p (j h) -> p j h", h=4), ACT.Tanh, scale=0.5)
            b = dve.do([b], V.tensor_scalar, beta, beta, 0.5, 0.5, ALU.mult, ALU.add)
            c = act.do([m, z], A.copy, cb[:, 0:8, 3:SEQ + 3], ps[:, 0, :].rearrange("p (n t) -> p n t", t=SEQ))
            c = act.do([m], A.copy, cb[:, 8:12, 3:SEQ + 3], ps[:, 1, 0:ST].rearrange("p (n t) -> p n t", t=SEQ))
            for k in range(3):
                o4 = acc[:, k * ST:(k + 1) * ST].rearrange("p (q t) -> p q t", q=SQ)
                a = None
                for tap in range(4):
                    src = cb[:, 4 * k:4 * k + 4, tap:tap + SEQ]
                    wt = wc("L3a_conv")[:, 4 * k + tap:4 * k + tap + 1]
                    if tap == 0:
                        a = dve.do([c], V.tensor_scalar, o4, src, wt, None, ALU.mult)
                    else:
                        a = dve.do([a], V.scalar_tensor_tensor, o4, src, wt, o4, ALU.mult, ALU.add)
            a = act.do([a], A.activation, th, acc, ACT.Tanh, scale=0.5)
            a = dve.do([a], V.scalar_tensor_tensor, s3, th, 1.0, acc, ALU.add, ALU.mult)
            a = dve.do([a], V.tensor_scalar, s3, s3, 0.5, None, ALU.mult)
            yield
            q_t, k_t, v_t = (s3[:, k * ST:(k + 1) * ST] for k in range(3))
            v4 = v_t.rearrange("p (q t) -> p q t", q=SQ)
            f = pool.do([a, z2], G.tensor_copy, vp[:, :, 63:127], v4)
            sq = acc[:, 0:512]
            s = act.do([a], A.square, sq, s3[:, 0:512])
            pe.wait(s)
            for k in range(2):
                for j in range(TS):
                    m = T.matmul(ps[:, 2, 16 + (k * TS + j) * 4:16 + (k * TS + j) * 4 + 4],
                                 lhsT=sq[:, k * ST + j * P:k * ST + (j + 1) * P], rhs=cc("headsel"), start=True, stop=True)
            m = pe.mark(m)
            ss = sc[:, 16:32].rearrange("p (k h j) -> p k h j", k=2, j=TS)
            r = dve.do([m], V.tensor_scalar, ss.rearrange("p k h j -> p k j h"),
                       ps[:, 2, 16:32].rearrange("p (k j h) -> p k j h", k=2, h=4), 1e-6, None, ALU.add)
            rr = sc[:, 32:48].rearrange("p (k h j) -> p k h j", k=2, j=TS)
            r2 = pool.do([r], G.tensor_tensor, sc[:, 32:48], sc[:, 16:32], bc(cc("half_neg")[:, 0], 1, 16), ALU.pow)
            dd = sc[:, 48:56].rearrange("p (h j) -> p h j", j=TS)
            br = sc[:, 56:64].rearrange("p (h j) -> p h j", j=TS)
            d = dve.do([r], V.reciprocal, dd, ss[:, 1, :, :])
            d = dve.do([d, b], V.tensor_tensor, dd, dd, beta, ALU.mult)
            b2 = dve.do([r2, b], V.tensor_tensor, br, rr[:, 1, :, :], beta, ALU.mult)
            first = True
            for n, (K, o) in enumerate(((3, 0), (15, 3), (64, 18))):
                f4 = fir[:, n * ST:(n + 1) * ST].rearrange("p (q t) -> p q t", q=SQ)
                for tap in range(K):
                    src = vp[:, :, 64 - K + tap:128 - K + tap]
                    wt = wc("L3a_fir")[:, o + tap:o + tap + 1]
                    if tap == 0:
                        fa = dve.do([f], V.tensor_scalar, f4, src, wt, None, ALU.mult)
                    else:
                        fa = dve.do([fa], V.scalar_tensor_tensor, f4, src, wt, f4, ALU.mult, ALU.add)
                yield
            pe.wait(fa)
            for j in range(TS):
                for n in range(4):
                    src = (fir[:, n * ST + j * P:n * ST + (j + 1) * P] if n < 3 else v_t[:, j * P:(j + 1) * P])
                    m = T.transpose(ps[:, j, n * P:(n + 1) * P], src, ident)
            m = pe.mark(m)
            for j in range(TS):
                p1 = act.do([m], A.copy, paths[:, j, 0:3, :], ps[:, j, 0:3 * P].rearrange("p (c n) -> p c n", c=3))
                p1 = act.do([m], A.copy, paths[:, j, 4, :], ps[:, j, 3 * P:4 * P])
                p2 = dve.do([m, b2, p1], V.tensor_tensor, bv[:, j, :].rearrange("p (h d) -> p h d", h=4),
                            ps[:, j, 3 * P:4 * P].rearrange("p (h d) -> p h d", h=4), bc(br[:, :, j], 2, 32), ALU.mult)
            yield
            gm = ar[:, D0:D0 + 1024].rearrange("p (h j n) -> p h j n", h=4, j=TS)
            gu = ar[:, D0 + 1024:D0 + 2048].rearrange("p (n k) -> p n k", k=P)
            tb = ar[:, D0 + 2048:D0 + 3072].rearrange("p (n k) -> p n k", k=P)
            pb = ar[:, D0 + 3072:D0 + 4096].rearrange("p (n k) -> p n k", k=P)
            tc, ttc, pc = (ar[:, D0 + 4096 + 256 * n:D0 + 4352 + 256 * n].rearrange("p (n k) -> p n k", k=32)
                           for n in range(3))
            yv, zv, wv = (ar[:, D0 + 4864 + 256 * n:D0 + 5120 + 256 * n].rearrange("p (n k) -> p n k", k=32)
                          for n in range(3))
            pe.wait(p1, p2)
            for j in range(TS):
                for h in range(4):
                    rows = slice(32 * h, 32 * h + 32)
                    m = T.matmul(ps[:, h, j * P:(j + 1) * P], lhsT=k_t[rows, j * P:(j + 1) * P],
                                 rhs=k_t[rows, j * P:(j + 1) * P], start=True, stop=True)
            m = pe.mark(m)
            g_ready = act.do([m, fa], A.copy, gm, ps[:, :, 0:ST].rearrange("p h (j n) -> p h j n", j=TS))
            g8 = gm.rearrange("p h j n -> p (h j) n")
            i32 = bc(cc("ident32"), 1, 8)
            t_ready = dve.do([fa], V.tensor_copy, tc, i32)
            tt_ready = dve.do([], V.tensor_copy, ttc, i32)
            tb_ready = dve.do([], V.tensor_copy, tb, bc(ident, 1, 8))
            dd8 = bc(sc[:, 48:56], 2, 32)
            blocks = bc(cc("blocks").rearrange("p (b k) -> p b k", b=4), 1, 8)
            yield
            prev = None
            for m_ in (1, 2, 4, 8, 16):
                u = pool.do([g_ready, prev], G.tensor_tensor, gu, g8, bc(cc(f"up{m_}"), 1, 8), ALU.mult)
                pe.wait(u, t_ready)
                for n in range(8):
                    m = T.matmul(ps[:, 0, n * 32:(n + 1) * 32], lhsT=gu[:, n, :], rhs=tc[:, n, :], start=True, stop=True)
                prev = m = pe.mark(m)
                a = dve.do([m], V.tensor_tensor, pc, ps[:, 0, 0:256].rearrange("p (n k) -> p n k", k=32), dd8, ALU.mult)
                e = dve.do([a], V.tensor_tensor, pb.rearrange("p n (b k) -> p n b k", b=4), bc(pc, 2, 4), blocks, ALU.mult)
                yield
                pe.wait(a, tb_ready)
                for n in range(8):
                    m = T.matmul(ps[:, 1, n * 32:(n + 1) * 32], lhsT=tb[:, n, :], rhs=pc[:, n, :], start=True, stop=True)
                mx_ = pe.mark(m)
                pe.wait(e, tt_ready)
                for n in range(8):
                    m = T.matmul(ps[:, 2, n * 32:(n + 1) * 32], lhsT=pb[:, n, :], rhs=ttc[:, n, :], start=True, stop=True)
                m = pe.mark(m)
                t_ready = dve.do([mx_], V.tensor_tensor, tc, tc, ps[:, 1, 0:256].rearrange("p (n k) -> p n k", k=32),
                                 ALU.subtract)
                tt_ready = dve.do([m], V.tensor_tensor, ttc, ttc, ps[:, 2, 0:256].rearrange("p (n k) -> p n k", k=32),
                                  ALU.subtract)
                tb_ready = dve.do([tt_ready], V.tensor_tensor, tb.rearrange("p n (b k) -> p n b k", b=4), bc(ttc, 2, 4),
                                  blocks, ALU.mult)
                yield
            u = pool.do([prev], G.tensor_tensor, gu, g8, bc(cc("up32"), 1, 8), ALU.mult)
            pe.wait(tb_ready, t_ready)
            for h in range(4):
                for j in range(TS):
                    n = h * TS + j
                    m = T.matmul(ps[:, 0, n * 32:(n + 1) * 32], lhsT=tb[:, n, :], rhs=bv[:, j, 32 * h:32 * h + 32],
                                 start=True, stop=True)
            m = pe.mark(m)
            a = dve.do([m], V.tensor_copy, yv, ps[:, 0, 0:256].rearrange("p (n k) -> p n k", k=32))
            pe.wait(a, u)
            for n in range(8):
                m = T.matmul(ps[:, 1, n * 32:(n + 1) * 32], lhsT=gu[:, n, :], rhs=yv[:, n, :], start=True, stop=True)
            m = pe.mark(m)
            a = dve.do([m], V.tensor_tensor, zv, ps[:, 1, 0:256].rearrange("p (n k) -> p n k", k=32), dd8, ALU.mult)
            yield
            pe.wait(a)
            for n in range(8):
                m = T.matmul(ps[:, 2, n * 32:(n + 1) * 32], lhsT=tb[:, n, :], rhs=zv[:, n, :], start=True, stop=True)
            m = pe.mark(m)
            a = dve.do([m], V.tensor_tensor, wv, yv, ps[:, 2, 0:256].rearrange("p (n k) -> p n k", k=32), ALU.subtract)
            pe.wait(a)
            for j in range(TS):
                for h in range(4):
                    rows = slice(32 * h, 32 * h + 32)
                    m = T.matmul(ps[:, h, j * P:(j + 1) * P], lhsT=k_t[rows, j * P:(j + 1) * P],
                                 rhs=q_t[rows, j * P:(j + 1) * P], start=True, stop=True)
            m = pe.mark(m)
            lt = pb
            a = dve.do([m], V.tensor_tensor, lt.rearrange("p (h j) n -> p h j n", h=4),
                       ps[:, :, 0:ST].rearrange("p h (j n) -> p h j n", j=TS), bc(bc(cc("within"), 1, TS), 1, 4), ALU.mult)
            yield
            pe.wait(a)
            for n in range(8):
                m = T.matmul(ps[:, 0, n * 32:(n + 1) * 32], lhsT=lt[:, n, :], rhs=wv[:, n, :], start=True, stop=True)
            m = pe.mark(m)
            for j in range(TS):
                a = dve.do([m], V.tensor_tensor, paths[:, j, 3, :].rearrange("p (h d) -> p h d", h=4),
                           ps[:, 0, 0:256].rearrange("p (h j d) -> p h j d", h=4, j=TS)[:, :, j, :],
                           bc(rr[:, 0, :, j], 2, 32), ALU.mult)
            yield
            pr = ar[:, D0:D0 + 1280]
            p4 = ar[:, 1536:2816].rearrange("p (n d) -> p n d", d=32)
            stt = sc[:, 320:480].rearrange("p (n s) -> p n s", s=4)
            raw3 = sc[:, 480:600].rearrange("p (s n) -> p s n", s=3)
            s_ = act.do([a], A.square, pr, ar[:, 1536:2816])
            b = dve.do([a], V.tensor_reduce, raw3[:, 0, :], p4, AX, ALU.add)
            c = dve.do([a], V.tensor_reduce, raw3[:, 2, :], p4, AX, ALU.add, apply_absolute_value=True)
            e = dve.do([s_], V.tensor_reduce, raw3[:, 1, :], pr.rearrange("p (n d) -> p n d", d=32), AX, ALU.add)
            for k, src in enumerate((b, e, c)):
                a = dve.do([src], V.tensor_scalar, stt[:, :, k], raw3[:, k, :], 1.0 / 32, None, ALU.mult)
            c = pool.do([e, a], G.tensor_tensor, stt[:, :, 3], raw3[:, 1, :], bc(cc("half_pos")[:, 0], 1, 40), ALU.pow)
            yield
            pe.wait(c, a)
            for j in range(TS):
                m = T.transpose(ps[0:80, 0, j * P:(j + 1) * P], sc[:, 320 + 80 * j:400 + 80 * j], ident)
            m = pe.mark(m)
            sT = ar[0:80, D0 + 1280:D0 + 1280 + ST]
            a = act.do([m], A.copy, sT, ps[0:80, 0, 0:ST])
            pe.wait(a)
            for c in range(2):
                T.matmul(ps[:, 1, c * ST:(c + 1) * ST], lhsT=wc("L3a_gW1")[:, c * P:(c + 1) * P], rhs=st.xt[:, :],
                         start=True, stop=False)
                m = T.matmul(ps[:, 1, c * ST:(c + 1) * ST], lhsT=G1S[0:80, c * P:(c + 1) * P], rhs=sT,
                             start=False, stop=True)
            m = pe.mark(m)
            yield
            hg = ar[:, D0 + 1536:D0 + 2048]
            for c in range(2):
                a = act.do([m], A.activation, hg[:, c * ST:(c + 1) * ST], ps[:, 1, c * ST:(c + 1) * ST], ACT.Gelu,
                           bias=wc("L3a_gb1")[:, c:c + 1])
            pe.wait(a)
            for j in range(TS):
                for c in range(2):
                    m = T.matmul(ps[:, 2, j * 32:j * 32 + 20], lhsT=hg[:, c * ST + j * P:c * ST + (j + 1) * P],
                                 rhs=wc("L3a_gW2")[:, c * 20:(c + 1) * 20], start=(c == 0), stop=(c == 1))
            m = pe.mark(m)
            lg = sc[:, 64:104].rearrange("p (j n) -> p j n", j=TS)
            lh = sc[:, 64:104].rearrange("p (n c) -> p n c", c=5)
            mx = sc[:, 104:112]
            a = dve.do([m], V.tensor_tensor, lg, ps[:, 2, 0:64].rearrange("p (j n) -> p j n", j=TS)[:, :, 0:20],
                       bc(wc("L3a_gb2"), 1, TS), ALU.add)
            a = dve.do([a], V.tensor_tensor, lg.rearrange("p j (h c) -> p j h c", c=5), lg.rearrange("p j (h c) -> p j h c", c=5),
                       bc(bc(PR5[:, 0:4], 2, 5), 1, TS), ALU.mult)
            a = dve.do([a], V.tensor_reduce, mx, lh, AX, ALU.max)
            a = dve.do([a], V.tensor_tensor, lh, lh, bc(mx, 2, 5), ALU.subtract)
            a = act.do([a], A.activation, lh, lh, ACT.Exp)
            yield
            a = dve.do([a], V.tensor_reduce, mx, lh, AX, ALU.add)
            a = dve.do([a], V.reciprocal, mx, mx)
            a = dve.do([a], V.tensor_tensor, mx.rearrange("p (j h) -> p j h", j=TS), mx.rearrange("p (j h) -> p j h", j=TS),
                       bc(PR5[:, 24:28], 1, TS), ALU.mult)
            a = dve.do([a], V.tensor_tensor, lh, lh, bc(mx, 2, 5), ALU.mult)
            a = dve.do([a], V.tensor_tensor, lg, lg, bc(PR5[:, 4:24], 1, TS), ALU.add)
            o_ = ar[:, D0 + 2048:D0 + 2304]
            for j in range(TS):
                prj = pr[:, 640 * j:640 * j + 640]
                pw = lg[:, j, :].rearrange("p (h c) -> p c h", c=5)
                b = dve.do([a], V.tensor_tensor, prj.rearrange("p (c h d) -> p c h d", c=5, h=4),
                           paths[:, j, :, :].rearrange("p c (h d) -> p c h d", h=4), bc(pw, 3, 32), ALU.mult)
                b = dve.do([b], V.tensor_reduce, o_[:, j * P:(j + 1) * P], prj.rearrange("p (c n) -> p n c", c=5), AX, ALU.add)
            yield
            oh = o_.rearrange("p (n d) -> p n d", d=32)
            sq2 = ar[:, D0 + 2304:D0 + 2560]
            a = act.do([b], A.square, sq2, o_)
            a = dve.do([a], V.tensor_reduce, mx, sq2.rearrange("p (n d) -> p n d", d=32), AX, ALU.add)
            a = dve.do([a], V.tensor_scalar, mx, mx, 1.0 / 32, 1e-5, ALU.mult, ALU.add)
            a = pool.do([a], G.tensor_tensor, mx, mx, bc(cc("half_neg")[:, 0], 1, 8), ALU.pow)
            a = dve.do([a], V.tensor_tensor, oh, oh, bc(mx, 2, 32), ALU.mult)
            a = dve.do([a], V.tensor_tensor, oh, oh, bc(wc("L3a_nw"), 1, 8), ALU.mult)
            pe.wait(a)
            for j in range(TS):
                m = T.transpose(ps[:, 3, j * P:(j + 1) * P], o_[:, j * P:(j + 1) * P], ident)
            m = pe.mark(m)
            a = act.do([m], A.copy, st.ot[:, :], ps[:, 3, 0:ST])
            yield
            pe.wait(a)
            for j in range(TS):
                m = T.matmul(ps[:, 3, ST + j * P:ST + (j + 1) * P], lhsT=st.ot[:, j * P:(j + 1) * P], rhs=wc("L3a_Wo"),
                             start=True, stop=True)
            m = pe.mark(m)
            st.done = dve.do([m], V.tensor_tensor, st.x[:, :, :], st.x[:, :, :],
                             ps[:, 3, ST:2 * ST].rearrange("p (j d) -> p j d", d=P), ALU.add)
            yield

        def alternate(gens, lag):
            live = [[k * lag, g] for k, g in enumerate(gens)]
            while live:
                for item in list(live):
                    if item[0] > 0:
                        item[0] -= 1
                    elif next(item[1], "end") == "end":
                        live.remove(item)

        def part_a(st, i):
            tiles = bass.ds(i * (NS * TS) + st.s * TS, TS)
            cols = bass.ds(i * (NS * ST) + st.s * ST, ST)
            st.done = dve.do([], V.tensor_copy, st.x[:, :, :], X[:, tiles, :])
            st.ct_ready = act.do([], A.copy, st.ct[:, :], CT[:, cols])
            yield from l0_attention(st)
            yield from attention(st, "L0x", wa, st.ct, masks=0)
            yield from l0_ffn(st)
            yield from attention(st, "L1a", wa, st.xt, masks=8, scale_v=wa("L1a_sv"), scale_o=wa("L1a_so"))
            yield from attention(st, "L1x", wa, st.ct, mix=wa("L1x_P"))
            dve.do([st.done], V.tensor_copy, X[:, tiles, :], st.x[:, :, :])
            yield from norm(st, st.done)
            a = act.do([st.normed], A.copy, XT[:, cols], st.xt[:, :])
            a = dve.do([a], V.tensor_reduce, st.sc[:, 4:5], st.xt[:, :], AX, ALU.max, apply_absolute_value=True)
            dve.do([a], V.tensor_tensor, SM[:, st.s:st.s + 1], SM[:, st.s:st.s + 1], st.sc[:, 4:5], ALU.max)

        zero = dve.do([], V.memset, SM[:, :], 0.0)
        act.wait(zero)
        drain_all()
        with nc.Fori(0, NITER) as i:
            alternate([part_a(st, i) for st in streams], 3)
            drain_all()

        U = flat[:, 0:6144].rearrange("p (k n) -> p k n", k=3)
        Gt = flat[:, 6144:12288].rearrange("p (k n) -> p k n", k=3)
        XQ = [flat[:, 12288 + 512 * n:12800 + 512 * n] for n in range(2)]
        TH = [flat[:, 13312 + 1536 * n:14848 + 1536 * n].rearrange("p (k n) -> p k n", k=3) for n in range(2)]
        NC = 4
        CH = NTOK // NC
        AM = sb("AM", [P, 16])
        SCB = sb("SCB", [P, 16])
        row = sb("row", [1, P])
        top = sb("top", [1, 1])
        bank = [PS[n // 4][:, n % 4, :] for n in range(8)]

        def global_scale(col, ready, dst, factor=None):
            pe.wait(ready)
            m = pe.mark(T.transpose(bank[7][0:1, 0:P], col, ident))
            a = dve.do([m], V.tensor_reduce, top[:, :], bank[7][0:1, 0:P], AX, ALU.max)
            pe.wait(a)
            m = pe.mark(T.matmul(bank[7][:, P:P + 1], lhsT=cc("one_row")[0:1, :], rhs=top[:, :], start=True, stop=True))
            if factor is None:
                a = dve.do([m], V.tensor_scalar, SCB[:, dst:dst + 1], bank[7][:, P:P + 1], float(1 / 32767.0), 1e-12,
                           ALU.mult, ALU.max)
            else:
                a = dve.do([m], V.tensor_scalar, SCB[:, dst:dst + 1], bank[7][:, P:P + 1], factor, float(1 / 32767.0),
                           ALU.mult, ALU.mult)
                a = dve.do([a], V.tensor_scalar, SCB[:, dst:dst + 1], SCB[:, dst:dst + 1], 1e-12, None, ALU.max)
            return dve.do([a], V.reciprocal, SCB[:, dst + 1:dst + 2], SCB[:, dst:dst + 1])

        def chunk(t, c):
            return t[:, :, c * CH:(c + 1) * CH]

        a = dve.do([], V.tensor_tensor, AM[:, 0:1], SM[:, 0:1], SM[:, 1:2], ALU.max)
        s0 = global_scale(AM[:, 0:1], a, 0)
        used = [None] * 2
        evac = [None] * 8
        nb = 0
        u_w, g_w = [None] * NC, [None] * NC
        for c in range(NC):
            xq = XQ[c % 2]
            a = dve.do([s0, used[c % 2]], V.tensor_scalar, xq, XT[:, c * CH:(c + 1) * CH], SCB[:, 1:2], RND,
                       ALU.mult, ALU.add)
            a = dve.do([a], V.tensor_scalar, xq, xq, RND, SCB[:, 0:1], ALU.subtract, ALU.mult)
            for k in range(6):
                pe.wait(a, evac[nb])
                m = pe.mark(T.matmul(bank[nb], lhsT=L1F[:, k, :], rhs=xq, start=True, stop=True))
                dst = (U if k < 3 else Gt)[:, k % 3, c * CH:(c + 1) * CH]
                evac[nb] = e = act.do([m], A.copy, dst, bank[nb])
                nb = (nb + 1) % 8
                if k == 2:
                    u_w[c] = e
            g_w[c] = e
            used[c % 2] = m
            dve.do([u_w[c]], V.tensor_reduce, AM[:, 1 + c:2 + c], chunk(U, c), mybir.AxisListType.XY, ALU.max,
                   apply_absolute_value=True)
            a = dve.do([g_w[c]], V.tensor_reduce, AM[:, 5 + c:6 + c], chunk(Gt, c), mybir.AxisListType.XY, ALU.max,
                       apply_absolute_value=True)
        a = dve.do([a], V.tensor_reduce, AM[:, 9:11], AM[:, 1:9].rearrange("p (a b) -> p a b", a=2), AX, ALU.max)
        pe.wait(*evac)
        su = global_scale(AM[:, 9:10], a, 2)
        sg = global_scale(AM[:, 10:11], su, 4)
        for c in range(NC):
            u, g, th_ = chunk(U, c), chunk(Gt, c), TH[c % 2]
            a = act.do([sg], A.activation, u, u, ACT.Identity, scale=SCB[:, 3:4], bias=cc("round"))
            u_w[c] = pool.do([a], G.tensor_scalar, u, u, RND, None, ALU.subtract)
            a = dve.do([sg], V.tensor_scalar, g, g, SCB[:, 5:6], RND, ALU.mult, ALU.add)
            a = dve.do([a], V.tensor_scalar, g, g, RND, SCB[:, 4:5], ALU.subtract, ALU.mult)
            a = act.do([a, g_w[c - 2] if c >= 2 else None], A.activation, th_, g, ACT.Tanh, scale=0.5)
            a = dve.do([a], V.tensor_scalar, th_, th_, 32768.0, 32768.0 + RND, ALU.mult, ALU.add)
            a = dve.do([a], V.tensor_scalar, th_, th_, RND, 65535.0, ALU.subtract, ALU.min)
            g_w[c] = dve.do([a], V.scalar_tensor_tensor, g, th_, 1.0 / 65536, g, ALU.mult, ALU.mult)
            a = dve.do([g_w[c]], V.tensor_reduce, AM[:, 1 + c:2 + c], g, mybir.AxisListType.XY, ALU.max,
                       apply_absolute_value=True)
        a = dve.do([a], V.tensor_reduce, AM[:, 9:10], AM[:, 1:5], AX, ALU.max)
        s3_ = global_scale(AM[:, 9:10], a, 6)
        sp = dve.do([s3_], V.tensor_tensor, SCB[:, 12:13], SCB[:, 6:7], SCB[:, 2:3], ALU.mult)
        for c in range(NC):
            u, g = chunk(U, c), chunk(Gt, c)
            a = act.do([s3_], A.activation, g, g, ACT.Identity, scale=SCB[:, 7:8], bias=cc("round"))
            a = dve.do([a, u_w[c]], V.scalar_tensor_tensor, g, g, RND, u, ALU.subtract, ALU.mult)
            a = dve.do([a], V.tensor_reduce, AM[:, 1 + c:2 + c], g, mybir.AxisListType.XY, ALU.max,
                       apply_absolute_value=True)
        a = dve.do([a], V.tensor_reduce, AM[:, 9:10], AM[:, 1:5], AX, ALU.max)
        s4 = global_scale(AM[:, 9:10], a, 8, factor=SCB[:, 12:13])
        s5 = dve.do([s4, sp], V.tensor_tensor, SCB[:, 10:11], SCB[:, 9:10], SCB[:, 12:13], ALU.mult)
        for c in range(NC):
            g = chunk(Gt, c)
            a = act.do([s5], A.activation, g, g, ACT.Identity, scale=SCB[:, 10:11], bias=cc("round"))
            a = dve.do([a], V.tensor_scalar, g, g, RND, None, ALU.subtract)
            pe.wait(a, evac[nb])
            for t in range(CH // P):
                for k in range(3):
                    o = c * CH + t * P
                    m = T.matmul(bank[nb][:, t * P:(t + 1) * P], lhsT=Gt[:, k, o:o + P], rhs=L1F[:, 6 + k, :],
                                 start=(k == 0), stop=(k == 2))
            m = pe.mark(m)
            xs = X[:, 4 * c:4 * c + 4, :]
            evac[nb] = dve.do([m], V.scalar_tensor_tensor, xs, bank[nb].rearrange("p (t d) -> p t d", d=P),
                              SCB[:, 8:9], xs, ALU.mult, ALU.add)
            nb = (nb + 1) % 8
        for e in (V, A, T, G):
            e.wait_ge(s_late, 16)
        drain_all()

        nc.sync.dma_start(stat, stat_d).then_inc(s_late, 16)
        mask_columns(16, wc, "L3x", False)
        rot8 = flat[0:8, 0:NTOK]
        done = None
        for k in range(4):
            pe.wait(done)
            for j in range(4):
                m = T.transpose(PS[0][0:8, 2, j * P:(j + 1) * P], sc8[:, 4 * k + j, :], ident)
            m = pe.mark(m)
            done = act.do([m], A.copy, rot8[:, 512 * k:512 * k + 512], PS[0][0:8, 2, :])
        for k in range(4):
            for c, sel in enumerate(("cos_sel", "sin_sel")):
                pe.wait(done)
                m = pe.mark(T.matmul(PS[0][:, c, :], lhsT=cc(sel)[0:8, :], rhs=rot8[:, 512 * k:512 * k + 512],
                                     start=True, stop=True))
                done = act.do([m], A.copy, ROT[:, c, 512 * k:512 * k + 512], PS[0][:, c, :])
        dve.do([], V.tensor_scalar, CN[:, :], CN[:, :], wc("L2x_mg"), wc("L2x_mb"), ALU.mult, ALU.add)
        ta = SM[:, 0:4]
        a = act.do([], A.activation, ta, wc("L3a_tau"), ACT.Abs)
        a = act.do([a], A.activation, ta, ta, ACT.Exp, scale=-1.0)
        a = act.do([a], A.activation, ta, ta, ACT.Ln, bias=1.0)
        a = dve.do([a], V.scalar_tensor_tensor, ta, wc("L3a_tau"), 0.0, ta, ALU.max, ALU.add)
        a = dve.do([a], V.tensor_scalar, ta, ta, 0.5, None, ALU.add)
        dve.do([a], V.reciprocal, PR5[:, 0:4], ta)
        a = act.do([], A.activation, PR5[:, 4:24], wc("L3a_eps"), ACT.Tanh, scale=0.5)
        a = dve.do([a], V.tensor_scalar, PR5[:, 4:24], PR5[:, 4:24], 0.1, 0.1, ALU.mult, ALU.add)
        a = dve.do([a], V.tensor_reduce, PR5[:, 28:32], PR5[:, 4:24].rearrange("p (h c) -> p h c", c=5), AX, ALU.add)
        dve.do([a], V.tensor_scalar, PR5[:, 24:28], PR5[:, 28:32], -1.0, 1.0, ALU.mult, ALU.add)
        T.wait_ge(s_late, 32)
        for n in range(20):
            m = T.matmul(PS[1][0:80, 0, 0:256], lhsT=cc("statsel")[:, 76 - 4 * n:156 - 4 * n],
                         rhs=stat[:, 256 * n:256 * n + 256], start=(n == 0), stop=(n == 19))
        m = pe.mark(m)
        act.do([m], A.copy, G1S[0:80, :], PS[1][0:80, 0, 0:256])
        drain_all()

        def part_c(st, i):
            tiles = bass.ds(i * (NS * TS) + st.s * TS, TS)
            cols = bass.ds(i * (NS * ST) + st.s * ST, ST)
            st.done = dve.do([], V.tensor_copy, st.x[:, :, :], X[:, tiles, :])
            st.ct_ready = act.do([], A.copy, st.ct[:, :], CT[:, cols])
            st.cn_ready = act.do([], A.copy, st.kvt[:, :, 0:SEQ], CN[:, cols].rearrange("p (q t) -> p q t", q=SQ))
            yield from l2_attention(st)
            yield from l2_cross(st)
            yield from l2_ffn(st)
            yield from l3_attention(st)
            yield from attention(st, "L3x", wc, st.ct, rope=(ROT[:, :, cols], st.done))
            yield from l3_ffn(st)
            dve.do([st.done], V.tensor_copy, X[:, tiles, :], st.x[:, :, :])

        with nc.Fori(0, NITER) as i:
            alternate([part_c(st, i) for st in streams], 3)
            drain_all()

        nc.sync.dma_start(out.rearrange("(t p) d -> p t d", p=P), X[:, :, :]).then_inc(s_out, 16)
        nc.sync.wait_ge(s_out, 16)


def kernel(**inputs):
    import numpy as np
    import concourse.bacc as bacc
    from concourse.bass_utils import run_bass_kernel_spmd as run

    t = {n: np.asarray(a) for n, a in inputs.items()}

    def rows(vec):
        return np.broadcast_to(np.reshape(vec, (1, -1)), (P, np.size(vec)))

    def col(vec):
        return np.reshape(vec, (P, 1))

    def chunks(a):
        return a.reshape(-1, P, a.shape[1]).transpose(1, 0, 2).reshape(P, -1)

    def pack(table, widths):
        parts = [table[n] for n, _ in widths]
        for p_, (n, w) in zip(parts, widths):
            assert p_.shape == (P, w), (n, p_.shape, w)
        return np.ascontiguousarray(np.concatenate(parts, axis=1))

    aw = {"L0a_gain": rows(t["L0_attn_gain"])}
    for n, src in (("L0x", "L0_xattn"), ("L1x", "L1_xattn"), ("L3x", "L3_xattn")):
        for m in "qkvo":
            aw[f"{n}_W{m}"] = t[f"{src}_W{m}"].T
            aw[f"{n}_b{m}"] = rows(t[f"{src}_bo"]) if m == "o" else col(t[f"{src}_b{m}"])
    for m in "qkvo":
        aw[f"L1a_W{m}"] = t[f"L1_attn_w_{m}"].T
        aw[f"L1a_b{m}"] = rows(t["L1_attn_b_o"]) if m == "o" else col(t[f"L1_attn_b_{m}"])
        aw[f"L1a_s{m}"] = rows(t[f"L1_attn_s_{m}"])
    aw["L1x_P"] = np.repeat(t["L1_xattn_P"], HD, axis=0)
    raw = {"L0a_w": np.concatenate([t[f"L0_attn_w_{m}"] for m in "qkvo"], axis=1),
           "L1f_w": np.concatenate([chunks(t["L1_ffn_w_up"]), chunks(t["L1_ffn_w_gate"]), t["L1_ffn_w_down"]], axis=1)}
    intw = np.ascontiguousarray(np.concatenate(
        [t["L0_ffn_w_gate"].T, t["L0_ffn_w_up"].T, chunks(t["L0_ffn_w_down"].T)], axis=1))
    swap = np.arange(P) ^ 4
    cw = dict(aw)
    cw["L3x_Wqp"], cw["L3x_Wkp"] = t["L3_xattn_Wq"].T[:, swap], t["L3_xattn_Wk"].T[:, swap]
    cw["L3x_bqp"], cw["L3x_bkp"] = col(t["L3_xattn_bq"][swap]), col(t["L3_xattn_bk"][swap])
    cw["L2a_w"], cw["L2a_Wo"] = t["L2_attn_w_attn"], t["L2_attn_w_proj"]
    for a_, b_ in (("mg", "ln_m_g"), ("mb", "ln_m_b"), ("lg", "ln_l_g"), ("lb", "ln_l_b")):
        cw[f"L2x_{a_}"] = col(t[f"L2_xattn_{b_}"])
    cw["L2x_Wq"], cw["L2x_Wkv"], cw["L2x_Wo"] = t["L2_xattn_Wq"], t["L2_xattn_Wkv"], chunks(t["L2_xattn_Wout"])
    cw["L2f_in"] = np.concatenate([t["L2_ffn_lora_A"].transpose(1, 0, 2).reshape(P, P), t["L2_ffn_router_w"].T], axis=1)
    cw["L2f_base"], cw["L2f_B"] = t["L2_ffn_base_w"].T, t["L2_ffn_lora_B"].reshape(P, P)
    cw["L2f_bb"], cw["L2f_rb"] = rows(t["L2_ffn_base_b"]), rows(t["L2_ffn_router_b"])
    a3 = {n[len("L3_attn_"):]: v for n, v in t.items() if n.startswith("L3_attn_")}
    cw["L3a_w"] = np.concatenate([a3["Wq"], a3["Wk"], a3["Wv"]], axis=1)
    cw["L3a_Wb"], cw["L3a_Wo"] = a3["Wb"], a3["Wo"]
    cw["L3a_conv"] = np.concatenate([a3["conv_q"], a3["conv_k"], a3["conv_v"]], axis=1)
    cw["L3a_fir"] = np.concatenate([a3["fir_s"], a3["fir_m"], a3["fir_l"]], axis=1)
    cw["L3a_gW1"] = a3["gW1"][0:P]
    cw["L3a_gb1"] = a3["gb1"].reshape(2, P).T
    cw["L3a_gW2"] = chunks(a3["gW2"])
    cw["L3a_gb2"], cw["L3a_tau"], cw["L3a_eps"] = rows(a3["gb2"]), rows(a3["log_tau"]), rows(a3["eps_logit"])
    cw["L3a_nw"] = rows(a3["norm_w"])
    f3 = {n[len("L3_ffn_"):]: v for n, v in t.items() if n.startswith("L3_ffn_")}
    cw["L3f_in"] = np.concatenate([f3["router_w"], f3["shared_gate_w"]], axis=1)
    cw["L3f_w1"] = f3["w1"].transpose(1, 0, 2).reshape(P, NE * P)
    cw["L3f_w2"] = f3["w2"].transpose(1, 0, 2).reshape(P, NE * P)
    cw["L3f_gu"], cw["L3f_down"] = f3["shared_gate_up"], f3["shared_down"]

    arrays = {
        "in_x": t["x"].reshape(NTOK, P), "in_ctx": t["ctx_1024"].reshape(NTOK, P),
        "in_coords": t["fside_BxSx3_0"].reshape(NTOK, 3),
        "in_const": np.ascontiguousarray(np.concatenate(list(constants().values()), axis=1)),
        "in_aw": pack(aw, A_W), "in_raw": pack(raw, RAW_W), "in_intw": intw, "in_cw": pack(cw, C_W),
        "in_stat": np.ascontiguousarray(chunks(a3["gW1"][P:])),
    }
    nc = bacc.Bacc("TRN2", target_bir_lowering=False, num_devices=1)
    aps = [nc.dram_tensor(n, a.shape, mybir.dt.from_np(a.dtype), kind="ExternalInput").ap() for n, a in arrays.items()]
    out = nc.dram_tensor("out_0", (NTOK, P), F32, kind="ExternalOutput").ap()
    decoder(nc, *aps, out)
    r = run(nc, [arrays], core_ids=[0])
    return r.results[0]["out_0"].reshape(B, SEQ, P)
```
